# Optimizing a Trainium2 kernel written in Bass

```python
import numpy as np
import jax
import jax.numpy as jnp

def _softmax(x, axis=-1):
    return jax.nn.softmax(x, axis=axis)

def _gelu(x):
    return jax.nn.gelu(x, approximate=True)

def _silu(x):
    return jax.nn.silu(x)

def _sigmoid(x):
    return jax.nn.sigmoid(x)

def _layernorm(x, axis=-1, eps=1e-05):
    m = jnp.mean(x, axis=axis, keepdims=True)
    v = jnp.var(x, axis=axis, keepdims=True)
    return (x - m) / jnp.sqrt(v + eps)

def _scatter_add(tgt, idx, src, axis=0):
    return tgt.at[idx].add(src)

def _segment_sum(src, seg, n):
    return jax.ops.segment_sum(src, seg, n)
kernel_name = 'mk_audio_tower_d1_tok_audfeat512_r4_bc9121'

def setup_inputs(seed: int=0):
    np.random.seed(seed)
    _w = jnp.asarray

    def _rec_inputs():
        import jax
        import jax.numpy as jnp
        _rk = jax.random.key(seed)
        x = 7.22013e-05 + 1.00017 * jax.random.normal(jax.random.fold_in(_rk, 1), (64, 375, 8), jnp.float32)
        return x
    x = _rec_inputs()

    def _L0_tok_setup():
        import jax, jax.numpy as jnp
        import numpy as np
        PATCH_LENGTH = 16
        STRIDE = 8
        D_MODEL = 128
        N_FEATURES = 8
        key = jax.random.key(seed)
        kx, kw, kb = jax.random.split(key, 3)
        x = jax.random.normal(kx, (64, 1024, N_FEATURES), dtype=jnp.float32)
        in_dim = PATCH_LENGTH * N_FEATURES
        bound = 1.0 / np.sqrt(in_dim)
        W = jax.random.uniform(kw, (in_dim, D_MODEL), dtype=jnp.float32, minval=-bound, maxval=bound)
        b = jax.random.uniform(kb, (D_MODEL,), dtype=jnp.float32, minval=-bound, maxval=bound)
        return {'x': x, 'W': W, 'b': b}
    _L0_tok_all = _L0_tok_setup()
    _L0_tok_in = {k: v for k, v in _L0_tok_all.items() if k in ('W', 'b')}
    del _L0_tok_all

    def _L0_attn_setup():
        import jax, jax.numpy as jnp
        import numpy as np
        HEADS = 8
        DIM = 128
        DH = DIM // HEADS
        M = DIM // 2
        PINV_ITERS = 6
        KER = 33
        EPS_LN = 1e-05

        def _moore_penrose_pinv(x, iters=PINV_ITERS):
            I = jnp.eye(x.shape[-1], dtype=x.dtype)
            denom = jnp.max(jnp.sum(jnp.abs(x), axis=-1)) * jnp.max(jnp.sum(jnp.abs(x), axis=-2))
            z = jnp.swapaxes(x, -1, -2) / denom
            for _ in range(iters):
                xz = x @ z
                z = 0.25 * z @ (13.0 * I - xz @ (15.0 * I - xz @ (7.0 * I - xz)))
            return z

        def _forward(x, gamma, beta, w_qkv, res_kernel, w_out, b_out):
            b, n, d = x.shape
            mu = jnp.mean(x, axis=-1, keepdims=True)
            var = jnp.var(x, axis=-1, keepdims=True)
            normed = (x - mu) / jnp.sqrt(var + EPS_LN) * gamma + beta
            pad = -n % M
            xp = jnp.pad(normed, ((0, 0), (pad, 0), (0, 0)))
            N = n + pad
            qkv = xp @ w_qkv
            q, k, v = jnp.split(qkv, 3, axis=-1)
            to_heads = lambda t: t.reshape(b, N, HEADS, DH).transpose(0, 2, 1, 3)
            q = to_heads(q) * DH ** (-0.5)
            k = to_heads(k)
            v = to_heads(v)
            l = N // M
            q_l = q.reshape(b, HEADS, M, l, DH).mean(axis=3)
            k_l = k.reshape(b, HEADS, M, l, DH).mean(axis=3)
            attn1 = jax.nn.softmax(jnp.einsum('bhnd,bhmd->bhnm', q, k_l), axis=-1)
            attn2 = jax.nn.softmax(jnp.einsum('bhmd,bhld->bhml', q_l, k_l), axis=-1)
            attn3 = jax.nn.softmax(jnp.einsum('bhmd,bhnd->bhmn', q_l, k), axis=-1)
            out = attn1 @ (_moore_penrose_pinv(attn2) @ (attn3 @ v))
            conv = jax.lax.conv_general_dilated(v, res_kernel, window_strides=(1, 1), padding=((KER // 2, KER // 2), (0, 0)), feature_group_count=HEADS, dimension_numbers=('NCHW', 'OIHW', 'NCHW'))
            out = out + conv
            out = out.transpose(0, 2, 1, 3).reshape(b, N, HEADS * DH)
            out = out @ w_out + b_out
            out = out[:, -n:]
            return x + out
        key = jax.random.key(seed)
        ks = jax.random.split(key, 5)
        b, n, d = (4, 2048, DIM)
        inner = HEADS * DH
        x = jax.random.normal(ks[0], (b, n, d), jnp.float32)
        gamma = jnp.ones((d,), jnp.float32)
        beta = jnp.zeros((d,), jnp.float32)
        w_qkv = jax.random.normal(ks[1], (d, inner * 3), jnp.float32) * d ** (-0.5)
        res_kernel = jax.random.normal(ks[2], (HEADS, 1, KER, 1), jnp.float32) * 0.1
        w_out = jax.random.normal(ks[3], (inner, d), jnp.float32) * inner ** (-0.5)
        b_out = jnp.zeros((d,), jnp.float32)
        return dict(x=x, gamma=gamma, beta=beta, w_qkv=w_qkv, res_kernel=res_kernel, w_out=w_out, b_out=b_out)
    _L0_attn_all = _L0_attn_setup()
    _L0_attn_in = {k: v for k, v in _L0_attn_all.items() if k in ('gamma', 'beta', 'w_qkv', 'res_kernel', 'w_out', 'b_out')}
    del _L0_attn_all

    def _L0_ffn_setup():
        import jax, jax.numpy as jnp
        import numpy as np
        B, S, H, E, K = (8, 1024, 128, 8, 2)
        key = jax.random.key(seed)
        ks = jax.random.split(key, 7)
        s_h = 1.0 / np.sqrt(H)
        s_2h = 1.0 / np.sqrt(2 * H)
        return {'x': jax.random.normal(ks[0], (B, S, H), dtype=jnp.float32), 'gate_w': jax.random.uniform(ks[1], (H, E), minval=-s_h, maxval=s_h, dtype=jnp.float32), 'gate_b': jax.random.uniform(ks[2], (E,), minval=-s_h, maxval=s_h, dtype=jnp.float32), 'w1': jax.random.uniform(ks[3], (E, H, 2 * H), minval=-s_h, maxval=s_h, dtype=jnp.float32), 'b1': jax.random.uniform(ks[4], (E, 2 * H), minval=-s_h, maxval=s_h, dtype=jnp.float32), 'w2': jax.random.uniform(ks[5], (E, 2 * H, H), minval=-s_2h, maxval=s_2h, dtype=jnp.float32), 'b2': jax.random.uniform(ks[6], (E, H), minval=-s_2h, maxval=s_2h, dtype=jnp.float32)}
    _L0_ffn_all = _L0_ffn_setup()
    _L0_ffn_in = {k: v for k, v in _L0_ffn_all.items() if k in ('gate_w', 'gate_b', 'w1', 'b1', 'w2', 'b2')}
    del _L0_ffn_all
    return {'x': x, 'L0_tok_W': _L0_tok_in['W'], 'L0_tok_b': _L0_tok_in['b'], 'L0_attn_gamma': _L0_attn_in['gamma'], 'L0_attn_beta': _L0_attn_in['beta'], 'L0_attn_w_qkv': _L0_attn_in['w_qkv'], 'L0_attn_res_kernel': _L0_attn_in['res_kernel'], 'L0_attn_w_out': _L0_attn_in['w_out'], 'L0_attn_b_out': _L0_attn_in['b_out'], 'L0_ffn_gate_w': _L0_ffn_in['gate_w'], 'L0_ffn_gate_b': _L0_ffn_in['gate_b'], 'L0_ffn_w1': _L0_ffn_in['w1'], 'L0_ffn_b1': _L0_ffn_in['b1'], 'L0_ffn_w2': _L0_ffn_in['w2'], 'L0_ffn_b2': _L0_ffn_in['b2']}

def reference(x, L0_tok_W, L0_tok_b, L0_attn_gamma, L0_attn_beta, L0_attn_w_qkv, L0_attn_res_kernel, L0_attn_w_out, L0_attn_b_out, L0_ffn_gate_w, L0_ffn_gate_b, L0_ffn_w1, L0_ffn_b1, L0_ffn_w2, L0_ffn_b2):
    import jax
    import jax.numpy as jnp

    def _L0_tok_ref(x, W, b):
        import jax, jax.numpy as jnp
        import numpy as np
        PATCH_LENGTH = 16
        STRIDE = 8
        D_MODEL = 128
        N_FEATURES = 8
        B, L, C = x.shape
        n_patches = (L - PATCH_LENGTH) // STRIDE + 1
        starts = jnp.arange(n_patches) * STRIDE
        idx = starts[:, None] + jnp.arange(PATCH_LENGTH)[None, :]
        patches = x[:, idx, :]
        patches = patches.reshape(B, n_patches, PATCH_LENGTH * C)
        out = jnp.einsum('bnk,kd->bnd', patches, W) + b
        return out

    def _L0_attn_ref(x, gamma, beta, w_qkv, res_kernel, w_out, b_out):
        import jax, jax.numpy as jnp
        import numpy as np
        HEADS = 8
        DIM = 128
        DH = DIM // HEADS
        M = DIM // 2
        PINV_ITERS = 6
        KER = 33
        EPS_LN = 1e-05

        def _moore_penrose_pinv(x, iters=PINV_ITERS):
            I = jnp.eye(x.shape[-1], dtype=x.dtype)
            denom = jnp.max(jnp.sum(jnp.abs(x), axis=-1)) * jnp.max(jnp.sum(jnp.abs(x), axis=-2))
            z = jnp.swapaxes(x, -1, -2) / denom
            for _ in range(iters):
                xz = x @ z
                z = 0.25 * z @ (13.0 * I - xz @ (15.0 * I - xz @ (7.0 * I - xz)))
            return z

        def _forward(x, gamma, beta, w_qkv, res_kernel, w_out, b_out):
            b, n, d = x.shape
            mu = jnp.mean(x, axis=-1, keepdims=True)
            var = jnp.var(x, axis=-1, keepdims=True)
            normed = (x - mu) / jnp.sqrt(var + EPS_LN) * gamma + beta
            pad = -n % M
            xp = jnp.pad(normed, ((0, 0), (pad, 0), (0, 0)))
            N = n + pad
            qkv = xp @ w_qkv
            q, k, v = jnp.split(qkv, 3, axis=-1)
            to_heads = lambda t: t.reshape(b, N, HEADS, DH).transpose(0, 2, 1, 3)
            q = to_heads(q) * DH ** (-0.5)
            k = to_heads(k)
            v = to_heads(v)
            l = N // M
            q_l = q.reshape(b, HEADS, M, l, DH).mean(axis=3)
            k_l = k.reshape(b, HEADS, M, l, DH).mean(axis=3)
            attn1 = jax.nn.softmax(jnp.einsum('bhnd,bhmd->bhnm', q, k_l), axis=-1)
            attn2 = jax.nn.softmax(jnp.einsum('bhmd,bhld->bhml', q_l, k_l), axis=-1)
            attn3 = jax.nn.softmax(jnp.einsum('bhmd,bhnd->bhmn', q_l, k), axis=-1)
            out = attn1 @ (_moore_penrose_pinv(attn2) @ (attn3 @ v))
            conv = jax.lax.conv_general_dilated(v, res_kernel, window_strides=(1, 1), padding=((KER // 2, KER // 2), (0, 0)), feature_group_count=HEADS, dimension_numbers=('NCHW', 'OIHW', 'NCHW'))
            out = out + conv
            out = out.transpose(0, 2, 1, 3).reshape(b, N, HEADS * DH)
            out = out @ w_out + b_out
            out = out[:, -n:]
            return x + out
        return _forward(x, gamma, beta, w_qkv, res_kernel, w_out, b_out)

    def _L0_ffn_ref(x, gate_w, gate_b, w1, b1, w2, b2):
        import jax, jax.numpy as jnp
        import numpy as np
        B, S, H, E, K = (8, 1024, 128, 8, 2)
        logits = jnp.einsum('bsh,he->bse', x, gate_w) + gate_b
        topk_vals, topk_idx = jax.lax.top_k(logits, K)
        topk_weights = jax.nn.softmax(topk_vals, axis=-1)
        mask = jax.nn.one_hot(topk_idx, E, dtype=topk_weights.dtype)
        weights = jnp.einsum('bske,bsk->bse', mask, topk_weights)
        h = jax.nn.relu(jnp.einsum('bsh,ehf->bsef', x, w1) + b1)
        expert_out = jnp.einsum('bsef,efh->bseh', h, w2) + b2
        return jnp.einsum('bseh,bse->bsh', expert_out, weights)
    h = _L0_tok_ref(x, L0_tok_W, L0_tok_b)
    h = h + _L0_attn_ref(_layernorm(h, axis=-1), L0_attn_gamma, L0_attn_beta, L0_attn_w_qkv, L0_attn_res_kernel, L0_attn_w_out, L0_attn_b_out)
    h = h + _L0_ffn_ref(_layernorm(h, axis=-1), L0_ffn_gate_w, L0_ffn_gate_b, L0_ffn_w1, L0_ffn_b1, L0_ffn_w2, L0_ffn_b2)
    return h

_drawn_inputs = setup_inputs


def setup_inputs(seed=0):
    import zlib

    import numpy as np

    out = dict(_drawn_inputs(seed))
    spreads = {'L0_attn_gamma': (1.0, 0.2), 'L0_attn_beta': (0.0, 0.1), 'L0_attn_b_out': (0.0, 0.1)}
    factors = {'L0_ffn_b1': 6.597, 'L0_ffn_b2': 3.63}
    for name, (base, spread) in spreads.items():
        noise = np.random.default_rng([zlib.crc32(name.encode()), seed]).standard_normal(out[name].shape)
        drawn = base * np.exp(spread * noise) if base else spread * noise
        out[name] = jnp.asarray(drawn.astype(out[name].dtype))
    for name, factor in factors.items():
        out[name] = (out[name] * factor).astype(out[name].dtype)
    return out
```

```python
import concourse.bass as bass
from concourse import mybir
from contextlib import ExitStack

F32 = mybir.dt.float32
U32 = mybir.dt.uint32
ALU = mybir.AluOpType
ACT = mybir.ActivationFunctionType
AX = mybir.AxisListType
RMAX = bass.bass_isa.ReduceOp.max

B, L, C = 64, 375, 8
PATCH, STRIDE = 16, 8
D = PATCH * C
NP = (L - PATCH) // STRIDE + 1
HEADS, DH = 8, 16
M = D // 2
PAD = -NP % M
KER = 33
ITERS = 6
EXPERTS, HID = 8, 256
EPS = 1e-5

NS = NP + 1
HALF = 64
BB = 8
UN = BB // 2
BLOCKS = B // BB
TT = 120
TILES = BB * NP // TT
BT = TILES * TT
BTP = BT + 8
GR = 4
SL = 2 * UN
NY = NS + DH
BW = SL * NS

PADW = float(PAD) ** 0.5
LAM = 3.0625
MU = LAM / 3.5
S_SCALE = 1.0 / (3.5 * LAM)
T_OUT = 0.6875 * LAM / MU
T_IN = 0.84375 / T_OUT

WARM = 5

CN_ME, CN_MO, CN_ROW, CN_COL, CN_EPS, CN_IOTA, CN_W = 128, 129, 130, 131, 132, 133, 144


def wait(eng, sem, value):
    if isinstance(value, int) and value <= 0:
        return
    eng.wait_ge(sem, value)


def wait_apart(eng, met, *waits):
    waits = [(s, v if isinstance(v, int) else eng.to_reg(v)) for s, v in waits]
    eng.wait_ge(*met)
    for s, v in waits:
        wait(eng, s, v)


class Steps:

    def __init__(self, eng, sem, per, met):
        self.eng, self.sem, self.per, self.met, self.base, self.k = eng, sem, per, met, 0, 0

    def start(self, block):
        self.base, self.k = block * self.per, 0

    def done(self, ins, apart=False):
        ins.then_inc(self.sem, 1)
        self.k += 1
        if apart:
            wait_apart(self.eng, self.met, (self.sem, self.base + self.k))
        else:
            self.eng.wait_ge(self.sem, self.base + self.k)

    def end(self):
        assert self.k == self.per, self.k


def patch_pieces():
    out = []
    for b in range(BB):
        n = 0
        while n < NP:
            t, p = divmod(b * NP + n, TT)
            c = min(NP - n, TT - p)
            out.append((t, p, b, n, c))
            n += c
    return out


def tower(nc, x, tok_w, tok_b, gamma, beta, w_qkv, res_k, w_out, b_out, gate_w, gate_b, w1, b1, w2, b2,
          consts, scratch, out):
    ctx = ExitStack()
    with ctx:
        def sb(name, shape, dt=F32):
            return ctx.enter_context(nc.sbuf_tensor(name, shape, dt))

        def sem(name):
            return ctx.enter_context(nc.semaphore(name))

        bank = [ctx.enter_context(nc.psum_tensor(f"bank{i}", [128, 512], F32)) for i in range(8)]

        cn = sb("cn", [128, CN_W])
        ident = cn[:, 0:128]
        tokw_sb = sb("tokw_sb", [D, D])
        tokb_sb = sb("tokb_sb", [128, D])
        bout_sb = sb("bout_sb", [128, D])
        gam_sb = sb("gam_sb", [D, 1])
        bet_sb = sb("bet_sb", [D, 1])
        wqkv_sb = sb("wqkv_sb", [D, 3 * D])
        wout_sb = sb("wout_sb", [D, D])
        kraw = sb("kraw", [HEADS, KER])
        kpad = sb("kpad", [HEADS, 2 * NP + 1])
        band = sb("band", [128, HEADS, NS])
        bands = sb("bands", [128, HEADS, NS])
        gw_sb = sb("gw_sb", [D, EXPERTS])
        gb_sb = sb("gb_sb", [128, EXPERTS])
        w1_sb = sb("w1_sb", [D, EXPERTS, HID])
        w2_sb = sb("w2_sb", [128, 2 * EXPERTS, D])
        b1_rows = sb("b1_rows", [2 * EXPERTS, 128])
        b1_sb = sb("b1_sb", [128, 2 * EXPERTS])
        b2_sb = sb("b2_sb", [EXPERTS, D])

        resid = sb("resid", [TT, BLOCKS * TILES, D])
        vals = sb("vals", [128, BLOCKS * UN, D])
        gram = sb("gram", [128, BLOCKS * GR * SL, NY])
        colsum = sb("colsum", [128, BLOCKS * GR * SL])
        rowsum = sb("rowsum", [128, BLOCKS * GR * SL])

        pat = sb("pat", [TT, TILES, D])
        patT = sb("patT", [D, BTP])
        h0 = sb("h0", [TT, TILES, D])
        h0b = sb("h0b", [TT, TILES, D])
        x1 = sb("x1", [TT, TILES, D])
        nm = sb("nm", [TT, TILES, D])
        stats = sb("stats", [TT, TILES, 6])
        mv = sb("mv", [TT, TILES, 2])
        sd = sb("sd", [TT, TILES])
        rstd = sb("rstd", [TT, TILES])
        normT = sb("normT", [D, BB, HALF])
        qeo = sb("qeo", [D, BB, 2, NS])
        kT = sb("kT", [D, BB, NS])
        E = [sb(f"E{i}", [128, SL, NS]) for i in range(2)]
        X = [sb(f"X{i}", [128, SL, HALF]) for i in range(2)]
        XT = [sb(f"XT{i}", [128, SL, NY]) for i in range(2)]
        mx = [sb(f"mx{i}", [128, SL]) for i in range(2)]
        r0 = sb("r0", [128, SL])
        cs0 = sb("cs0", [128, SL])
        rs = [sb(f"rs{i}", [128, SL]) for i in range(2)]
        ri = [sb(f"ri{i}", [128, SL]) for i in range(2)]
        rx = [sb(f"rx{i}", [128, SL]) for i in range(2)]
        cmax = sb("cmax", [128, 1])
        den = sb("den", [128, 2])
        den2 = sb("den2", [128, 2])
        dprod = sb("dprod", [128, 1])
        drec = sb("drec", [128, 1])
        lamc = sb("lamc", [128, 1])

        P0 = [sb(f"P0{g}", [128, SL, NS]) for g in range(GR)]
        P0Z = [sb(f"P0Z{g}", [128, SL, NS]) for g in range(GR)]
        P = [sb(f"P{g}", [128, SL, NS]) for g in range(GR)]
        Y = [sb(f"Y{g}", [128, SL, NS]) for g in range(GR)]
        W = [sb(f"W{g}", [128, SL, NS]) for g in range(GR)]
        PZ = [sb(f"PZ{g}", [128, SL, NS]) for g in range(GR)]
        WZ = [sb(f"WZ{g}", [128, SL, NS]) for g in range(GR)]
        T = [sb(f"T{g}", [128, SL, NS]) for g in range(GR)]
        vblk = sb("vblk", [128, UN, D])
        O = sb("O", [128, UN, D])
        OT = sb("OT", [D, BTP])

        xn = nm
        stats2, mv2, sd2, rstd2 = stats, mv, sd, rstd
        xnT = sb("xnT", [D, BTP])
        lg = sb("lg", [TT, TILES, EXPERTS])
        top = sb("top", [TT, TILES, 8])
        topi = sb("topi", [TT, TILES, 8], U32)
        topf = sb("topf", [TT, TILES, 8])
        oh1 = sb("oh1", [TT, TILES, EXPERTS])
        oh2 = sb("oh2", [TT, TILES, EXPERTS])
        dl = sb("dl", [TT, TILES, EXPERTS])
        ex = sb("ex", [TT, TILES, EXPERTS])
        em = sb("em", [TT, TILES, EXPERTS])
        es = sb("es", [TT, TILES])
        er = sb("er", [TT, TILES])
        wt = sb("wt", [TT, TILES, EXPERTS])
        wT = sb("wT", [EXPERTS, BTP])
        hT = [[sb(f"hT{i}{f}", [128, BTP]) for f in range(2)] for i in range(2)]
        acc = sb("acc", [TT, TILES, D])
        outb = sb("outb", [TT, TILES, D])

        s_cn, s_wa, s_wb, s_wc = sem("s_cn"), sem("s_wa"), sem("s_wb"), sem("s_wc")
        s_kraw, s_kpad, s_scr, s_band, s_bands = sem("s_kraw"), sem("s_kpad"), sem("s_scr"), sem("s_band"), sem("s_bands")
        s_init, s_psum = sem("s_init"), sem("s_psum")
        s_pat, s_pt, s_patT, s_h, s_h0 = sem("s_pat"), sem("s_pt"), sem("s_patT"), sem("s_h"), sem("s_h0")
        s_mv, s_sd, s_x1, s_res = sem("s_mv"), sem("s_sd"), sem("s_x1"), sem("s_res")
        s_nm, s_nt, s_normT = sem("s_nm"), sem("s_nt"), sem("s_normT")
        s_q, s_k, s_v, s_qk, s_vals, s_vx = sem("s_q"), sem("s_k"), sem("s_v"), sem("s_qk"), sem("s_vals"), sem("s_vx")
        s_s, s_sub, s_ex, s_norm, s_x = sem("s_s"), sem("s_sub"), sem("s_ex"), sem("s_norm"), sem("s_x")
        s_xt, s_xte, s_g, s_gram, s_cs = sem("s_xt"), sem("s_xte"), sem("s_g"), sem("s_gram"), sem("s_cs")
        s_d1, s_d2, s_hb = sem("s_d1"), sem("s_d2"), sem("s_hb")
        s_den, s_den2, s_lamc, s_dd, s_dmax, s_es = (sem("s_den"), sem("s_den2"), sem("s_lamc"), sem("s_dd"),
                                                      sem("s_dmax"), sem("s_es"))
        s_p0 = [sem(f"s_p0{g}") for g in range(GR)]
        s_p = [sem(f"s_p{g}") for g in range(GR)]
        s_pp = [sem(f"s_pp{g}") for g in range(GR)]
        s_w = [sem(f"s_w{g}") for g in range(GR)]
        s_pz = [sem(f"s_pz{g}") for g in range(GR)]
        s_wz = [sem(f"s_wz{g}") for g in range(GR)]
        s_t = [sem(f"s_t{g}") for g in range(GR)]
        s_ww = [sem(f"s_ww{g}") for g in range(GR)]
        s_y = [sem(f"s_y{g}") for g in range(GR)]
        s_r = [sem(f"s_r{g}") for g in range(GR)]
        s_o = [sem(f"s_o{g}") for g in range(GR)]
        s_vb, s_ot, s_OT, s_pr, s_h1 = sem("s_vb"), sem("s_ot"), sem("s_OT"), sem("s_pr"), sem("s_h1")
        s_b1t, s_b1 = sem("s_b1t"), sem("s_b1")
        s_mv2, s_sd2, s_xn, s_xnt, s_xnT = sem("s_mv2"), sem("s_sd2"), sem("s_xn"), sem("s_xnt"), sem("s_xnT")
        s_gt, s_dl, s_exg, s_wt, s_wtt, s_wT, s_b2, s_acc = (sem("s_gt"), sem("s_dl"), sem("s_exg"), sem("s_wt"),
                                                            sem("s_wtt"), sem("s_wT"), sem("s_b2"), sem("s_acc"))
        s_up, s_hT, s_dn, s_mix, s_d3, s_d4, s_out = (sem("s_up"), sem("s_hT"), sem("s_dn"), sem("s_mix"), sem("s_d3"),
                                               sem("s_d4"), sem("s_out"))
        N_WA, N_WB, N_WC = 6, 2, 6
        N_INIT = 11 + 3 * GR

        halves = [(0, NS), (HALF, HALF + NS)]
        pieces = patch_pieces()
        block = ctx.enter_context(nc.Block())

        def over_blocks(eng, body):
            body(0)
            with eng.Fori(1, BLOCKS - 1) as blk:
                body(blk)
            body(BLOCKS - 1)

        def rows3(ap, blk, n):
            return ap[:, bass.ds(blk * n, n), :]

        @block.sync
        def _(sp):
            def load_patches(blk):
                wait(sp, s_pt, blk)
                for t, p, b, n, c in pieces:
                    src = bass.AP(tensor=x.tensor, offset=(blk * BB + b) * (L * C) + n * STRIDE * C,
                                  ap=[[STRIDE * C, c], [1, D]])
                    sp.dma_start(pat[p:p + c, t, :], src).then_inc(s_pat, 16)

            load_patches(0)
            sp.dma_start(kraw[:, :], res_k.rearrange("h a k b -> h (a k b)")).then_inc(s_kraw, 16)
            sp.wait_ge(s_kpad, 2)
            sp.dma_start(scratch[:, :], kpad[:, :]).then_inc(s_scr, 16)
            sp.wait_ge(s_scr, 16)
            for lo, _ in halves:
                src = bass.AP(tensor=scratch.tensor, offset=0, ap=[[1, NS], [2 * NP + 1, HEADS], [1, NS]])
                sp.dma_start(band[lo:lo + NS, :, :], src).then_inc(s_band, 16)
            load_patches(1)
            with sp.Fori(2, BLOCKS) as blk:
                load_patches(blk)
            out_rows = out.rearrange("b n d -> (b n) d")

            def store(blk):
                sp.wait_ge(s_mix, 8 * blk + 8)
                sp.dma_start(out_rows[bass.ds(blk * BT, BT), :].rearrange("(t p) d -> p t d", p=TT),
                             outb[:, :, :]).then_inc(s_out, 16)

            store(0)
            with sp.Fori(1, BLOCKS) as blk:
                store(blk)
            sp.wait_ge(s_out, 16 * BLOCKS)

        @block.gpsimd
        def _(pool):
            pool.dma_start(gw_sb[:, :], gate_w).then_inc(s_wc, 16)
            pool.dma_start(gb_sb[:, :], gate_b.partition_broadcast(128)).then_inc(s_wc, 16)
            pool.dma_start(w1_sb[:, :, :], w1.rearrange("e h f -> h e f")).then_inc(s_wc, 16)
            pool.dma_start(w2_sb[:, :, :], w2.rearrange("e (c f) h -> f (e c) h", c=2)).then_inc(s_wc, 16)
            pool.dma_start(b1_rows[:, :], b1.rearrange("e (c f) -> (e c) f", c=2)).then_inc(s_wc, 16)
            pool.dma_start(b2_sb[:, :], b2).then_inc(s_wc, 16)
            for t in (normT[:, :, :], X[0][:, :, :], X[1][:, :, :], patT[:, BT:BTP], xnT[:, BT:BTP], OT[:, BT:BTP],
                      wT[:, BT:BTP], hT[0][0][:, BT:BTP], hT[0][1][:, BT:BTP], hT[1][0][:, BT:BTP],
                      hT[1][1][:, BT:BTP]) + tuple(z[:, :, :] for z in P0Z + PZ + WZ):
                pool.memset(t, 0.0).then_inc(s_init, 1)

            def residual(blk):
                pool.wait_ge(s_h0, blk + 1)
                pool.tensor_tensor(out=h0b[:, :, :], in0=h0[:, :, :],
                                   in1=bout_sb[0:TT, :].unsqueeze(1).broadcast_to([TT, TILES, D]),
                                   op=ALU.add).then_inc(s_hb, 1)
                pool.wait_ge(s_hb, blk + 1)
                pool.wait_ge(s_x1, blk + 1)
                pool.tensor_tensor(out=rows3(resid, blk, TILES), in0=h0b[:, :, :], in1=x1[:, :, :],
                                   op=ALU.add).then_inc(s_res, 1)

            def values(blk, g):
                i = blk * GR + g
                pool.wait_ge(s_vals, blk + 1)
                wait(pool, s_g, i - 1)
                src = vals[:, bass.ds(blk * UN, UN), 2 * DH * g:2 * DH * (g + 1)]
                pool.tensor_copy(XT[g % 2][:, :, NS:NY].rearrange("p (u a) d -> p u a d", a=2),
                                 src.rearrange("p u (a d) -> p u a d", a=2)).then_inc(s_vx, 1)

            def scale_rows(blk, g):
                i = blk * GR + g
                pool.wait_ge(s_norm, i + 1)
                wait(pool, s_xt, i - 1)
                pool.tensor_tensor(out=X[g % 2][:, :, 0:NS], in0=E[g % 2][:, :, :],
                                   in1=rx[g % 2][:, :].unsqueeze(2).broadcast_to([128, SL, NS]),
                                   op=ALU.mult).then_inc(s_x, 1)
                pool.tensor_tensor(out=rowsum[:, bass.ds(i * SL, SL)], in0=rs[g % 2][:, :],
                                   in1=ri[g % 2][:, :], op=ALU.mult).then_inc(s_d2, 1)

            pool.wait_ge(s_init, N_INIT)
            pool.wait_ge(s_wa, 16 * N_WA)
            residual(0)

            def body(blk, more=True):
                values(blk, 0)
                scale_rows(blk, 0)
                values(blk, 1)
                scale_rows(blk, 1)
                values(blk, 2)
                if more:
                    residual(blk + 1)
                scale_rows(blk, 2)
                values(blk, 3)
                scale_rows(blk, 3)

            body(0)
            with pool.Fori(1, BLOCKS - 1) as blk:
                body(blk)
            body(BLOCKS - 1, False)

            pool.wait_ge(s_den, 2)
            pool.partition_all_reduce(den2[:, :], den[:, :], 128, RMAX).then_inc(s_den2, 1)

            def block_values(blk):
                for g in range(GR):
                    wait(pool, s_r[g], blk)
                    pool.tensor_copy(Y[g][:, :, :], rows3(gram, blk * GR + g, SL)[:, :, NY - NS:NY]).then_inc(s_y[g], 1)
                wait(pool, s_r[GR - 1], blk)
                pool.tensor_copy(vblk[:, :, :], rows3(vals, blk, UN)).then_inc(s_vb, 1)

            def next_p(blk):
                for g in range(GR):
                    wait(pool, s_t[g], ITERS * (blk - 1) + 1)
                    src = rows3(gram, blk * GR + g, SL)
                    scale = lamc[:, 0:1].unsqueeze(2).broadcast_to([128, SL, NS])
                    pool.tensor_tensor(out=P0[g][:, :, :], in0=src[:, :, 0:NS], in1=scale, op=ALU.mult).then_inc(s_p0[g], 1)
                    pool.tensor_tensor(out=P0Z[g][0:HALF, :, :], in0=src[0:HALF, :, 0:NS], in1=scale[0:HALF],
                                       op=ALU.mult).then_inc(s_p0[g], 1)

            block_values(0)
            pool.wait_ge(s_lamc, 1)
            with pool.Fori(1, BLOCKS) as blk:
                next_p(blk)
                block_values(blk)

        @block.scalar
        def _(act):
            act.dma_start(cn[:, :], consts).then_inc(s_cn, 16)
            act.dma_start(tokw_sb[:, :], tok_w).then_inc(s_wa, 16)
            act.dma_start(tokb_sb[:, :], tok_b.partition_broadcast(128)).then_inc(s_wa, 16)
            act.dma_start(bout_sb[:, :], b_out.partition_broadcast(128)).then_inc(s_wa, 16)
            act.dma_start(gam_sb[:, :], gamma.unsqueeze(1)).then_inc(s_wa, 16)
            act.dma_start(bet_sb[:, :], beta.unsqueeze(1)).then_inc(s_wa, 16)
            act.dma_start(wqkv_sb[:, :], w_qkv).then_inc(s_wa, 16)
            act.dma_start(wout_sb[:, :], w_out).then_inc(s_wb, 16)

            def patches(blk):
                act.wait_ge(s_pt, blk + 1)
                wait(act, s_h, blk)
                act.activation(patT[:, 0:BT], bank[0][:, 0:BT], ACT.Copy).then_inc(s_patT, 1)

            def root(blk, j):
                act.wait_ge(s_mv, 2 * blk + j + 1)
                act.activation(sd[:, :], mv[:, :, 1], ACT.Sqrt, bias=cn[0:TT, CN_EPS:CN_EPS + 1]).then_inc(s_sd, 1)

            def normed(blk):
                act.wait_ge(s_nt, blk + 1)
                wait(act, s_v, blk)
                act.activation(normT[:, :, 1:NS], bank[0][:, 0:BT].rearrange("p (b n) -> p b n", b=BB),
                               ACT.Identity, bias=bet_sb[:, 0:1], scale=gam_sb[:, 0:1]).then_inc(s_normT, 1)

            def qkv(blk):
                q = bank[2][:, 0:BW].rearrange("p (b n) -> p b n", b=BB)
                act.wait_ge(s_q, blk + 1)
                act.activation(qeo[:, :, 0, :], q, ACT.Copy, scale=cn[:, CN_ME:CN_ME + 1]).then_inc(s_qk, 1)
                act.activation(qeo[:, :, 1, :], q, ACT.Copy, scale=cn[:, CN_MO:CN_MO + 1]).then_inc(s_qk, 1)
                act.wait_ge(s_k, blk + 1)
                act.activation(kT[:, :, :], bank[3][:, 0:BW].rearrange("p (b n) -> p b n", b=BB),
                               ACT.Copy).then_inc(s_qk, 1)
                act.wait_ge(s_v, blk + 1)
                act.activation(rows3(vals, blk, UN), bank[0][:, :].rearrange("p (u d) -> p u d", u=UN),
                               ACT.Copy).then_inc(s_vals, 1)

            def exps(blk, g):
                act.wait_ge(s_sub, blk * GR + g + 1)
                act.activation(E[g % 2][:, :, :], E[g % 2][:, :, :], ACT.Exp).then_inc(s_ex, 1)

            def xt_out(blk, g):
                i = blk * GR + g
                act.wait_ge(s_xt, i + 1)
                wait(act, s_cs, i - 1)
                wait(act, s_g, i - 1)
                act.activation(XT[g % 2][:, :, 0:NS],
                               bank[6][:, :].rearrange("p (s n) -> p s n", s=SL)[:, :, 0:NS],
                               ACT.Copy).then_inc(s_xte, 1)

            def gram_out(blk, g):
                i = blk * GR + g
                act.wait_ge(s_g, i + 1)
                act.activation(rows3(gram, i, SL), bank[7][:, 0:SL * NY].rearrange("p (s n) -> p s n", s=SL),
                               ACT.Copy).then_inc(s_gram, 1)

            act.wait_ge(s_cn, 16)
            act.wait_ge(s_wa, 16 * N_WA)
            act.wait_ge(s_init, N_INIT)
            patches(0)
            root(0, 0)
            root(0, 1)
            normed(0)

            def body(blk, more=True):
                qkv(blk)
                exps(blk, 0)
                if more:
                    patches(blk + 1)
                exps(blk, 1)
                xt_out(blk, 0)
                if more:
                    root(blk + 1, 0)
                gram_out(blk, 0)
                xt_out(blk, 1)
                exps(blk, 2)
                gram_out(blk, 1)
                if more:
                    root(blk + 1, 1)
                exps(blk, 3)
                xt_out(blk, 2)
                gram_out(blk, 2)
                xt_out(blk, 3)
                if more:
                    normed(blk + 1)
                gram_out(blk, 3)

            body(0)
            with act.Fori(1, BLOCKS - 1) as blk:
                body(blk)
            body(BLOCKS - 1, False)

            act.wait_ge(s_b1t, 1)
            act.activation(b1_sb[:, :], bank[6][:, 0:2 * EXPERTS], ACT.Copy).then_inc(s_b1, 1)
            act.wait_ge(s_lamc, 1)

            def first_p(blk):
                for g in range(GR):
                    src = rows3(gram, blk * GR + g, SL)
                    act.activation(P0[g][:, :, :], src[:, :, 0:NS], ACT.Copy, scale=lamc[:, 0:1]).then_inc(s_p0[g], 1)
                    act.activation(P0Z[g][0:HALF, :, :], src[0:HALF, :, 0:NS], ACT.Copy,
                                   scale=lamc[0:HALF, 0:1]).then_inc(s_p0[g], 1)

            def over_zeros(src, dst, sem_in, sem_out, count):
                for g in range(GR):
                    act.wait_ge(sem_in[g], count)
                    act.activation(dst[g][0:HALF, :, :], src[g][0:HALF, :, :], ACT.Copy).then_inc(sem_out[g], 1)

            def attention_rows(blk):
                act.wait_ge(s_ot, blk + 1)
                act.activation(OT[:, 0:BT].rearrange("p (b n) -> p b n", b=BB),
                               bank[4][:, :].rearrange("p (b n) -> p b n", b=BB)[:, :, 1:NS],
                               ACT.Copy).then_inc(s_OT, 1)

            def b_body(blk, before=True):
                over_zeros(W, WZ, s_w, s_wz, blk * ITERS + 1)
                if before:
                    attention_rows(blk - 1)
                over_zeros(P, PZ, s_p, s_pz, blk * ITERS + 1)
                with act.Fori(1, ITERS) as k:
                    over_zeros(W, WZ, s_w, s_wz, blk * ITERS + k + 1)
                    over_zeros(P, PZ, s_p, s_pz, blk * ITERS + k + 1)

            first_p(0)
            b_body(0, False)
            with act.Fori(1, BLOCKS) as blk:
                b_body(blk)
            attention_rows(BLOCKS - 1)

            def root2(blk):
                act.wait_ge(s_mv2, blk + 1)
                act.activation(sd2[:, :], mv2[:, :, 1], ACT.Sqrt, bias=cn[0:TT, CN_EPS:CN_EPS + 1]).then_inc(s_sd2, 1)

            def xn_out(blk):
                act.wait_ge(s_xnt, blk + 1)
                act.activation(xnT[:, 0:BT], bank[0][:, 0:BT], ACT.Copy).then_inc(s_xnT, 1)

            def relus(blk, e):
                for f in range(2):
                    j = blk * 16 + 2 * e + f
                    act.wait_ge(s_up, j + 1)
                    wait(act, s_dn, blk * 8 + e - 1)
                    act.activation(hT[e % 2][f][:, 0:BT], bank[4 + f][:, 0:BT], ACT.Relu,
                                   bias=b1_sb[:, 2 * e + f:2 * e + f + 1]).then_inc(s_hT, 1)

            root2(0)
            xn_out(0)

            def c_body(blk, more=True):
                relus(blk, 0)
                act.wait_ge(s_dl, blk + 1)
                act.activation(ex[:, :, :], dl[:, :, :], ACT.Exp).then_inc(s_exg, 1)
                relus(blk, 1)
                act.wait_ge(s_wtt, blk + 1)
                act.activation(wT[:, 0:BT], bank[2][0:EXPERTS, 0:BT], ACT.Copy).then_inc(s_wT, 1)
                for e in range(2, 6):
                    relus(blk, e)
                if more:
                    root2(blk + 1)
                relus(blk, 6)
                relus(blk, 7)
                if more:
                    xn_out(blk + 1)

            c_body(0)
            with act.Fori(1, BLOCKS - 1) as blk:
                c_body(blk)
            c_body(BLOCKS - 1, False)

        @block.vector
        def _(dve):
            for bk in bank:
                dve.memset(bk[:, :], 0.0).then_inc(s_psum, 1)
            dve.memset(kpad[:, :], 0.0).then_inc(s_kpad, 1)
            dve.wait_ge(s_kraw, 16)
            dve.wait_ge(s_kpad, 1)
            first = NP - KER // 2
            dve.tensor_copy(kpad[:, first:first + KER], kraw[:, :]).then_inc(s_kpad, 1)
            a1 = Steps(dve, s_d1, 4, (s_cn, 16))
            a2 = Steps(dve, s_dd, 4 * 6, (s_cn, 16))
            dve.wait_ge(s_cn, 16)
            dve.wait_ge(s_wa, 16 * N_WA)

            def ln_stats(src, st, m, chain):
                for t in range(TILES):
                    ins = dve.bn_stats(st[:, t, :], src(t))
                chain.done(ins, True)
                for t in range(TILES):
                    ins = dve.bn_aggr(m[:, t, :], st[:, t, :])
                return ins

            def ln_apply(dst, src, m, r):
                for t in range(TILES):
                    ins = dve.tensor_scalar(dst[:, t, :], src(t), m[:, t, 0:1], r[:, t:t + 1],
                                            ALU.subtract, ALU.mult)
                return ins

            def embed(blk):
                a1.start(blk)
                dve.wait_ge(s_h, blk + 1)
                wait(dve, s_res, blk)
                dve.tensor_tensor(out=h0[:, :, :],
                                  in0=bank[1][0:TT, 0:TILES * D].rearrange("p (t d) -> p t d", t=TILES),
                                  in1=tokb_sb[0:TT, :].unsqueeze(1).broadcast_to([TT, TILES, D]),
                                  op=ALU.add).then_inc(s_h0, 1)
                dve.wait_ge(s_h0, blk + 1)
                ln_stats(lambda t: h0[:, t, :], stats, mv, a1).then_inc(s_mv, 1)

            def first_norm(blk):
                dve.wait_ge(s_sd, 2 * blk + 1)
                a1.done(dve.reciprocal(rstd[:, :], sd[:, :]))
                ln_apply(x1, lambda t: h0[:, t, :], mv, rstd).then_inc(s_x1, 1)
                dve.wait_ge(s_x1, blk + 1)
                ln_stats(lambda t: x1[:, t, :], stats, mv, a1).then_inc(s_mv, 1)

            def second_norm(blk):
                dve.wait_ge(s_sd, 2 * blk + 2)
                a1.done(dve.reciprocal(rstd[:, :], sd[:, :]))
                wait(dve, s_nt, blk)
                ln_apply(nm, lambda t: x1[:, t, :], mv, rstd).then_inc(s_nm, 1)

            def subtract(blk, g):
                i = blk * GR + g
                S = bank[4 + g % 2][:, 0:BW].rearrange("p (s n) -> p s n", s=SL)
                dve.wait_ge(s_s, i + 1)
                a2.done(dve.reduce_max(mx[g % 2][:, :], S, AX.X))
                wait(dve, s_x, i - 1)
                dve.tensor_tensor(out=E[g % 2][:, :, :], in0=S,
                                  in1=mx[g % 2][:, :].unsqueeze(2).broadcast_to([128, SL, NS]),
                                  op=ALU.subtract).then_inc(s_sub, 1)

            def normalise(blk, g):
                i = blk * GR + g
                e, b = E[g % 2], g % 2
                dve.wait_ge(s_ex, i + 1)
                wait(dve, s_d2, i - 1)
                a2.done(dve.reduce_sum(r0[:, :], e[:, :, :], AX.X))
                a2.done(dve.scalar_tensor_tensor(out=rs[b][:, :], in0=e[:, :, 0], scalar=float(PAD - 1),
                                                 in1=r0[:, :], op0=ALU.mult, op1=ALU.add))
                a2.done(dve.reciprocal(ri[b][:, :], rs[b][:, :]))
                a2.done(dve.tensor_scalar(rx[b][:, :], ri[b][:, :], cn[:, CN_ROW:CN_ROW + 1], None, ALU.mult))
                dve.tensor_scalar(e[:, :, 0], e[:, :, 0], PADW, None, ALU.mult).then_inc(s_norm, 1)

            def columns(blk, g):
                i = blk * GR + g
                dve.wait_ge(s_xte, i + 1)
                a2.done(dve.reduce_sum(cs0[:, :], XT[g % 2][:, :, 0:NS], AX.X))
                dve.scalar_tensor_tensor(out=colsum[:, bass.ds(i * SL, SL)], in0=XT[g % 2][:, :, 0],
                                         scalar=PADW - 1.0, in1=cs0[:, :], op0=ALU.mult,
                                         op1=ALU.add).then_inc(s_cs, 1)
                dve.wait_ge(s_cs, i + 1)

            def body(blk, more=True):
                a2.start(blk)
                subtract(blk, 0)
                subtract(blk, 1)
                normalise(blk, 0)
                if more:
                    embed(blk + 1)
                normalise(blk, 1)
                columns(blk, 0)
                subtract(blk, 2)
                if more:
                    first_norm(blk + 1)
                columns(blk, 1)
                normalise(blk, 2)
                subtract(blk, 3)
                if more:
                    second_norm(blk + 1)
                    a1.end()
                normalise(blk, 3)
                columns(blk, 2)
                columns(blk, 3)
                a2.end()

            embed(0)
            first_norm(0)
            second_norm(0)
            a1.end()
            body(0)
            with dve.Fori(1, BLOCKS - 1) as blk:
                body(blk)
            body(BLOCKS - 1, False)

            dve.wait_ge(s_vals, BLOCKS)
            dve.wait_ge(s_qk, 3 * BLOCKS)
            for g in range(GR):
                dve.memset(bank[g][:, :], 0.0).then_inc(s_psum, 1)
            dve.reduce_max(cmax[:, :], colsum[:, :], AX.X).then_inc(s_dmax, 1)
            dve.wait_ge(s_d2, BLOCKS * GR)
            dve.reduce_max(den[:, 1:2], rowsum[:, :], AX.X).then_inc(s_den, 1)
            dve.wait_ge(s_dmax, 1)
            dve.tensor_scalar(den[:, 0:1], cmax[:, :], cn[:, CN_COL:CN_COL + 1], None, ALU.mult).then_inc(s_den, 1)
            dve.wait_ge(s_den2, 1)
            dve.tensor_tensor(out=dprod[:, :], in0=den2[:, 0:1], in1=den2[:, 1:2], op=ALU.mult).then_inc(s_dmax, 1)
            dve.wait_ge(s_dmax, 2)
            dve.reciprocal(drec[:, :], dprod[:, :]).then_inc(s_dmax, 1)
            dve.wait_ge(s_dmax, 3)
            dve.tensor_scalar(lamc[:, :], drec[:, :], LAM, None, ALU.mult).then_inc(s_lamc, 1)
            dve.wait_ge(s_band, 16 * 2)
            for lo, hi in halves:
                dve.tensor_scalar(bands[lo:hi, :, :], band[lo:hi, :, ::-1], LAM, None, ALU.mult).then_inc(s_bands, 1)

            def psum3(k, n):
                return bank[k][:, 0:SL * n].rearrange("p (s n) -> p s n", s=SL)

            def step(blk, k, src):
                c = blk * ITERS + k
                for g in range(GR):
                    dve.wait_ge(s_pp[g], c + 1)
                    dve.scalar_tensor_tensor(out=W[g][:, :, :], in0=psum3(g, NS), scalar=S_SCALE,
                                             in1=src[g][:, :, :], op0=ALU.mult, op1=ALU.subtract).then_inc(s_w[g], 1)
                    dve.wait_ge(s_w[g], c + 1)
                    dve.scalar_tensor_tensor(out=T[g][:, :, :], in0=src[g][:, :, :], scalar=T_IN, in1=W[g][:, :, :],
                                             op0=ALU.mult, op1=ALU.subtract).then_inc(s_t[g], 1)
                for g in range(GR):
                    dve.wait_ge(s_ww[g], c + 1)
                    dve.wait_ge(s_t[g], c + 1)
                    dve.scalar_tensor_tensor(out=P[g][:, :, :], in0=T[g][:, :, :], scalar=T_OUT, in1=psum3(g, NS),
                                             op0=ALU.mult, op1=ALU.subtract).then_inc(s_p[g], 1)

            def h1(blk):
                dve.wait_ge(s_pr, blk + 1)
                r = rows3(resid, blk, TILES)
                dve.tensor_tensor(out=r, in0=bank[5][0:TT, 0:TILES * D].rearrange("p (t d) -> p t d", t=TILES),
                                  in1=r, op=ALU.add).then_inc(s_h1, 1)

            def attention_out(blk):
                for g in range(GR):
                    dve.wait_ge(s_r[g], blk + 1)
                    dve.tensor_scalar(
                        O[:, :, 2 * DH * g:2 * DH * (g + 1)].rearrange("p u (a d) -> p u a d", a=2),
                        bank[4 + g][:, 0:BW].rearrange("p (u a n) -> p u a n", u=UN, a=2)[:, :, :, NS - DH:NS],
                        1.0 / LAM, None, ALU.mult).then_inc(s_o[g], 1)

            def b_body(blk, before=True):
                step(blk, 0, P0)
                if before:
                    h1(blk - 1)
                with dve.Fori(1, ITERS) as k:
                    step(blk, k, P)
                attention_out(blk)

            b_body(0, False)
            with dve.Fori(1, BLOCKS) as blk:
                b_body(blk)
            h1(BLOCKS - 1)
            dve.wait_ge(s_h1, BLOCKS)

            c1 = Steps(dve, s_d3, 2, (s_cn, 16))
            c2 = Steps(dve, s_d4, 8, (s_cn, 16))

            def third_norm(blk):
                c1.start(blk)
                r = rows3(resid, blk, TILES)
                ln_stats(lambda t: r[:, t, :], stats2, mv2, c1).then_inc(s_mv2, 1)
                dve.wait_ge(s_sd2, blk + 1)
                c1.done(dve.reciprocal(rstd2[:, :], sd2[:, :]))
                wait(dve, s_xnt, blk)
                ln_apply(xn, lambda t: r[:, t, :], mv2, rstd2).then_inc(s_xn, 1)
                c1.end()

            def every(ap, n):
                return ap.unsqueeze(2).broadcast_to([TT, TILES, n])

            def gate(blk):
                c2.start(blk)
                dve.wait_ge(s_gt, blk + 1)
                wait(dve, s_mix, 8 * blk)
                c2.done(dve.tensor_tensor(
                    out=lg[:, :, :], in0=bank[1][0:TT, 0:TILES * EXPERTS].rearrange("p (t e) -> p t e", t=TILES),
                    in1=gb_sb[0:TT, :].unsqueeze(1).broadcast_to([TT, TILES, EXPERTS]), op=ALU.add), True)
                for t in range(TILES):
                    ins = dve.max(top[:, t, :], lg[:, t, :])
                c2.done(ins)
                dve.tensor_tensor(out=dl[:, :, :], in0=lg[:, :, :], in1=every(top[:, :, 0], EXPERTS),
                                  op=ALU.subtract).then_inc(s_dl, 1)
                for t in range(TILES):
                    ins = dve.max_index(topi[:, t, :], top[:, t, :], lg[:, t, :])
                c2.done(ins)
                c2.done(dve.tensor_copy(topf[:, :, :], topi[:, :, :]))
                places = cn[0:TT, CN_IOTA:CN_IOTA + EXPERTS].unsqueeze(1).broadcast_to([TT, TILES, EXPERTS])
                dve.tensor_tensor(out=oh1[:, :, :], in0=places, in1=every(topf[:, :, 0], EXPERTS), op=ALU.is_equal)
                c2.done(dve.tensor_tensor(out=oh2[:, :, :], in0=places, in1=every(topf[:, :, 1], EXPERTS),
                                          op=ALU.is_equal))
                c2.done(dve.tensor_tensor(out=oh1[:, :, :], in0=oh1[:, :, :], in1=oh2[:, :, :], op=ALU.add))
                dve.wait_ge(s_exg, blk + 1)
                c2.done(dve.tensor_tensor(out=em[:, :, :], in0=ex[:, :, :], in1=oh1[:, :, :], op=ALU.mult))
                dve.reduce_sum(es[:, :], em[:, :, :], AX.X).then_inc(s_es, 1)
                dve.wait_ge(s_es, blk + 1)
                c2.done(dve.reciprocal(er[:, :], es[:, :]))
                dve.tensor_tensor(out=wt[:, :, :], in0=em[:, :, :], in1=every(er[:, :], EXPERTS),
                                  op=ALU.mult).then_inc(s_wt, 1)
                c2.end()

            def start_sum(blk):
                dve.wait_ge(s_b2, blk + 1)
                dve.tensor_tensor(out=acc[:, :, :],
                                  in0=bank[3][0:TT, 0:TILES * D].rearrange("p (t d) -> p t d", t=TILES),
                                  in1=rows3(resid, blk, TILES), op=ALU.add).then_inc(s_acc, 1)

            def mix(blk, e):
                j = blk * EXPERTS + e
                dve.wait_ge(s_dn, j + 1)
                if e == 0:
                    dve.wait_ge(s_acc, blk + 1)
                    dve.wait_ge(s_wt, blk + 1)
                else:
                    dve.wait_ge(s_mix, j)
                dst = acc
                if e == EXPERTS - 1:
                    dst = outb
                    wait(dve, s_out, 16 * blk)
                y = bank[6 + e % 2][0:TT, 0:TILES * D].rearrange("p (t d) -> p t d", t=TILES)
                for t in range(TILES):
                    ins = dve.scalar_tensor_tensor(out=dst[:, t, :], in0=y[:, t, :], scalar=wt[:, t, e:e + 1],
                                                   in1=acc[:, t, :], op0=ALU.mult, op1=ALU.add)
                ins.then_inc(s_mix, 1)

            third_norm(0)

            def c_body(blk, more=True):
                gate(blk)
                start_sum(blk)
                for e in range(6):
                    mix(blk, e)
                if more:
                    third_norm(blk + 1)
                mix(blk, 6)
                mix(blk, 7)

            c_body(0)
            with dve.Fori(1, BLOCKS - 1) as blk:
                c_body(blk)
            c_body(BLOCKS - 1, False)

        @block.tensor
        def _(pe):
            def mm(out, lhsT, rhs, start=True, stop=True):
                return pe.matmul(out, lhsT, rhs, start=start, stop=stop, skip_group_check=True)

            met = (s_cn, 16)
            pe.wait_ge(s_psum, 8)
            pe.wait_ge(s_init, N_INIT)
            pe.wait_ge(s_cn, 16)

            def patches(blk):
                pe.wait_ge(s_pat, 16 * len(pieces) * blk + 16 * len(pieces))
                wait(pe, s_vals, blk)
                for t in range(TILES):
                    ins = pe.transpose(bank[0][:, t * TT:(t + 1) * TT], pat[:, t, :], ident[0:TT, 0:TT])
                ins.then_inc(s_pt, 1)

            def embed(blk):
                pe.wait_ge(s_patT, blk + 1)
                wait(pe, s_h0, blk)
                for t in range(TILES):
                    ins = mm(bank[1][:, t * D:(t + 1) * D], patT[:, t * TT:t * TT + 128], tokw_sb[:, :])
                ins.then_inc(s_h, 1)

            def normed(blk):
                pe.wait_ge(s_nm, blk + 1)
                for t in range(TILES):
                    ins = pe.transpose(bank[0][:, t * TT:(t + 1) * TT], nm[:, t, :], ident[0:TT, 0:TT])
                ins.then_inc(s_nt, 1)

            def qkv(blk):
                pe.wait_ge(s_normT, blk + 1)
                rhs = normT[:, :, 0:NS]
                mm(bank[2][:, 0:BW].rearrange("p (b n) -> p b n", b=BB), wqkv_sb[:, 0:D], rhs).then_inc(s_q, 1)
                mm(bank[3][:, 0:BW].rearrange("p (b n) -> p b n", b=BB), wqkv_sb[:, D:2 * D], rhs).then_inc(s_k, 1)
                for u in range(UN):
                    ins = mm(bank[0][:, u * D:(u + 1) * D], normT[:, 2 * u:2 * u + 2, :].rearrange("p b n -> p (b n)"),
                             wqkv_sb[:, 2 * D:3 * D])
                ins.then_inc(s_v, 1)

            def scores(blk, g):
                i = blk * GR + g
                if g == 0:
                    pe.wait_ge(s_qk, 3 * blk + 3)
                wait(pe, s_sub, i - 1)
                r = slice(32 * g, 32 * g + 32)
                for b in range(BB):
                    for a, (lo, hi) in enumerate(halves):
                        ins = pe.matmul(bank[4 + g % 2][lo:hi, b * NS:(b + 1) * NS], qeo[r, b, a, :], kT[r, b, :],
                                        start=True, stop=True, skip_group_check=True, tile_position=(32 * g, lo))
                ins.then_inc(s_s, 1)

            def turn(blk, g):
                i = blk * GR + g
                pe.wait_ge(s_x, i + 1)
                wait(pe, s_xte, i)
                for u in range(UN):
                    ins = pe.transpose(bank[6][:, u * 128:(u + 1) * 128],
                                       X[g % 2][:, 2 * u:2 * u + 2, :].rearrange("p b n -> p (b n)"), ident)
                ins.then_inc(s_xt, 1)

            def products(blk, g):
                i = blk * GR + g
                wait_apart(pe, met, (s_xte, i + 1), (s_vx, i + 1), (s_gram, i))
                for s in range(SL):
                    for lo, hi in halves:
                        ins = mm(bank[7][lo:hi, s * NY:(s + 1) * NY], XT[g % 2][lo:lo + HALF, s, 0:NS],
                                 XT[g % 2][lo:lo + HALF, s, :])
                ins.then_inc(s_g, 1)

            pe.wait_ge(s_wa, 16 * N_WA)
            patches(0)
            embed(0)
            normed(0)

            def body(blk, more=True):
                qkv(blk)
                scores(blk, 0)
                if more:
                    patches(blk + 1)
                scores(blk, 1)
                if more:
                    embed(blk + 1)
                turn(blk, 0)
                products(blk, 0)
                scores(blk, 2)
                turn(blk, 1)
                products(blk, 1)
                scores(blk, 3)
                turn(blk, 2)
                products(blk, 2)
                if more:
                    normed(blk + 1)
                turn(blk, 3)
                products(blk, 3)

            body(0)
            with pe.Fori(1, BLOCKS - 1) as blk:
                body(blk)
            body(BLOCKS - 1, False)

            pe.wait_ge(s_wc, 16 * N_WC)
            pe.wait_ge(s_wb, 16)
            pe.transpose(bank[6][:, 0:2 * EXPERTS], b1_rows[:, :], ident[0:16, 0:16]).then_inc(s_b1t, 1)
            for _ in range(WARM):
                mm(bank[5][:, :], ident, w1_sb[:, 0:2, :].rearrange("p e f -> p (e f)"))

            def pair(out_bank, s, t, tz, rhs, **flags):
                mm(out_bank[0:NS, s * NS:(s + 1) * NS], tz[:, s, :], rhs, **flags)
                return mm(out_bank[HALF:HALF + NS, s * NS:(s + 1) * NS], t[HALF:128, s, :], rhs[HALF:128, :], **flags)

            def squares(g, t, tz):
                for s in range(SL):
                    ins = pair(bank[g], s, t, tz, t[:, s, :])
                return ins

            def p_squares(blk, k):
                for g in range(GR):
                    wait_apart(pe, met, (s_pz[g], blk * ITERS + k))
                    squares(g, P[g], PZ[g]).then_inc(s_pp[g], 1)

            def w_squares(blk, k):
                for g in range(GR):
                    wait_apart(pe, met, (s_wz[g], blk * ITERS + k + 1))
                    squares(g, W[g], WZ[g]).then_inc(s_ww[g], 1)

            def first_squares(blk):
                for g in range(GR):
                    wait_apart(pe, met, (s_p0[g], 2 * blk + 2))
                    squares(g, P0[g], P0Z[g]).then_inc(s_pp[g], 1)

            def turn_out(blk):
                for g in range(GR):
                    pe.wait_ge(s_o[g], blk + 1)
                for u in range(UN):
                    ins = pe.transpose(bank[4][:, u * 128:(u + 1) * 128], O[:, u, :], ident)
                ins.then_inc(s_ot, 1)

            def project(blk):
                pe.wait_ge(s_OT, blk + 1)
                for t in range(TILES):
                    ins = mm(bank[5][:, t * D:(t + 1) * D], OT[:, t * TT:t * TT + 128], wout_sb[:, :])
                ins.then_inc(s_pr, 1)

            def results(blk):
                for g in range(GR):
                    wait_apart(pe, met, (s_pz[g], ITERS * blk + ITERS), (s_y[g], blk + 1), (s_vb, blk + 1),
                               (s_h1, blk), (s_o[g], blk))
                    for s in range(SL):
                        pair(bank[4 + g], s, P[g], PZ[g], Y[g][:, s, :], start=(s == 0), stop=False)
                    for lo, hi in halves:
                        for a in range(2):
                            h = 2 * g + a
                            dst = bank[4 + g][lo:hi, 0:BW].rearrange("p (u a n) -> p u a n", u=UN, a=2)
                            ins = mm(dst[:, :, a, NS - DH:NS], bands[lo:hi, h, :], vblk[lo:hi, :, h * DH:(h + 1) * DH],
                                     start=False, stop=True)
                    ins.then_inc(s_r[g], 1)

            def b_body(blk, before=True):
                first_squares(blk)
                if before:
                    turn_out(blk - 1)
                w_squares(blk, 0)
                if before:
                    project(blk - 1)
                with pe.Fori(1, ITERS) as k:
                    p_squares(blk, k)
                    w_squares(blk, k)
                results(blk)

            pe.wait_ge(s_bands, 2)
            pe.wait_ge(s_psum, 8 + GR)
            b_body(0, False)
            with pe.Fori(1, BLOCKS) as blk:
                b_body(blk)
            turn_out(BLOCKS - 1)
            project(BLOCKS - 1)

            def third_norm(blk):
                pe.wait_ge(s_xn, blk + 1)
                for t in range(TILES):
                    ins = pe.transpose(bank[0][:, t * TT:(t + 1) * TT], xn[:, t, :], ident[0:TT, 0:TT])
                ins.then_inc(s_xnt, 1)

            def gate(blk):
                pe.wait_ge(s_xnT, blk + 1)
                for t in range(TILES):
                    ins = mm(bank[1][:, t * EXPERTS:(t + 1) * EXPERTS], xnT[:, t * TT:t * TT + 128], gw_sb[:, :])
                ins.then_inc(s_gt, 1)

            def up(blk, e):
                for f in range(2):
                    wait(pe, s_hT, blk * 16 + 2 * e + f - 1)
                    mm(bank[4 + f][:, 0:BT], w1_sb[:, e, f * 128:(f + 1) * 128], xnT[:, 0:BT]).then_inc(s_up, 1)

            def weights(blk):
                pe.wait_ge(s_wt, blk + 1)
                for t in range(TILES):
                    ins = pe.transpose(bank[2][0:EXPERTS, t * TT:(t + 1) * TT], wt[:, t, :], ident[0:TT, 0:TT])
                ins.then_inc(s_wtt, 1)

            def second_bias(blk):
                pe.wait_ge(s_wT, blk + 1)
                wait(pe, s_acc, blk)
                for t in range(TILES):
                    ins = mm(bank[3][:, t * D:(t + 1) * D], wT[:, t * TT:t * TT + 128], b2_sb[:, :])
                ins.then_inc(s_b2, 1)

            def down(blk, e):
                j = blk * EXPERTS + e
                pe.wait_ge(s_hT, 2 * j + 2)
                wait(pe, s_mix, j - 1)
                for t in range(TILES):
                    for f in range(2):
                        ins = mm(bank[6 + e % 2][:, t * D:(t + 1) * D], hT[e % 2][f][:, t * TT:t * TT + 128],
                                 w2_sb[:, 2 * e + f, :], start=(f == 0), stop=(f == 1))
                ins.then_inc(s_dn, 1)

            third_norm(0)
            gate(0)

            def c_body(blk, more=True):
                up(blk, 0)
                up(blk, 1)
                weights(blk)
                down(blk, 0)
                second_bias(blk)
                for e in range(2, EXPERTS):
                    up(blk, e)
                    down(blk, e - 1)
                if more:
                    third_norm(blk + 1)
                down(blk, EXPERTS - 1)
                if more:
                    gate(blk + 1)

            c_body(0)
            with pe.Fori(1, BLOCKS - 1) as blk:
                c_body(blk)
            c_body(BLOCKS - 1, False)


_INS = ['x', 'L0_tok_W', 'L0_tok_b', 'L0_attn_gamma', 'L0_attn_beta', 'L0_attn_w_qkv', 'L0_attn_res_kernel',
        'L0_attn_w_out', 'L0_attn_b_out', 'L0_ffn_gate_w', 'L0_ffn_gate_b', 'L0_ffn_w1', 'L0_ffn_b1',
        'L0_ffn_w2', 'L0_ffn_b2']


def shape_constants():
    import numpy as np
    cn = np.zeros((128, CN_W), np.float32)
    cn[:, 0:128] = np.eye(128)
    p = np.arange(128)
    cn[:, CN_ME] = np.where(p // DH % 2 == 0, DH ** -0.5, 0.0)
    cn[:, CN_MO] = np.where(p // DH % 2 == 1, DH ** -0.5, 0.0)
    cn[:, CN_ROW] = np.where(p % HALF == 0, PADW, 1.0)
    cn[:, CN_COL] = np.where(p % HALF == 0, 1.0 / PADW, np.where(p % HALF < NS, 1.0, 0.0))
    cn[:, CN_EPS] = EPS
    cn[:, CN_IOTA:CN_IOTA + EXPERTS] = np.arange(EXPERTS)
    return cn


def kernel(**inputs):
    import numpy as _np
    import concourse.bacc as _bacc
    from concourse.bass_utils import run_bass_kernel_spmd as _run

    nc = _bacc.Bacc("TRN2", target_bir_lowering=False, num_devices=1)
    arrays, args = {}, []
    for name in _INS:
        a = _np.ascontiguousarray(inputs[name])
        arrays[f"in_{name}"] = a
        args.append(nc.dram_tensor(f"in_{name}", a.shape, F32, kind="ExternalInput").ap())
    arrays["in_consts"] = shape_constants()
    consts = nc.dram_tensor("in_consts", (128, CN_W), F32, kind="ExternalInput").ap()
    scratch = nc.dram_tensor("scratch", (HEADS, 2 * NP + 1), F32, kind="Internal").ap()
    out = nc.dram_tensor("out", (B, NP, D), F32, kind="ExternalOutput").ap()
    tower(nc, *args, consts, scratch, out)
    r = _run(nc, [arrays], core_ids=[0])
    return r.results[0]["out"]
```

```python
import concourse.bass as bass
from concourse import mybir
from contextlib import ExitStack

F32 = mybir.dt.float32
U32 = mybir.dt.uint32
ALU = mybir.AluOpType
ACT = mybir.ActivationFunctionType
AX = mybir.AxisListType
RMAX = bass.bass_isa.ReduceOp.max

B, L, C = 64, 375, 8
PATCH, STRIDE = 16, 8
D = PATCH * C
NP = (L - PATCH) // STRIDE + 1
HEADS, DH = 8, 16
M = D // 2
PAD = -NP % M
KER = 33
ITERS = 6
EXPERTS, HID = 8, 256
EPS = 1e-5

NS = NP + 1
HALF = 64
BB = 8
UN = BB // 2
BLOCKS = B // BB
TT = 120
TILES = BB * NP // TT
BT = TILES * TT
BTP = BT + 8
GR = 4
SL = 2 * UN
NY = NS + DH
BW = SL * NS

PADW = float(PAD) ** 0.5
LAM = 3.0625
MU = LAM / 3.5
S_SCALE = 1.0 / (3.5 * LAM)
T_OUT = 0.6875 * LAM / MU
T_IN = 0.84375 / T_OUT

WARM_A, WARM_B = 1, 5

CN_ME, CN_MO, CN_ROW, CN_COL, CN_EPS, CN_EPS2, CN_IOTA, CN_W = 128, 129, 130, 131, 132, 133, 134, 144


def wait(eng, sem, value):
    if isinstance(value, int) and value <= 0:
        return
    eng.wait_ge(sem, value)


def wait_apart(eng, met, *waits):
    waits = [(s, v if isinstance(v, int) else eng.to_reg(v)) for s, v in waits]
    eng.wait_ge(*met)
    for s, v in waits:
        wait(eng, s, v)


class Steps:

    def __init__(self, eng, sem, per, met):
        self.eng, self.sem, self.per, self.met, self.base, self.k = eng, sem, per, met, 0, 0

    def start(self, block):
        self.base, self.k = block * self.per, 0

    def done(self, ins, apart=False):
        ins.then_inc(self.sem, 1)
        self.k += 1
        if apart:
            wait_apart(self.eng, self.met, (self.sem, self.base + self.k))
        else:
            self.eng.wait_ge(self.sem, self.base + self.k)

    def end(self):
        assert self.k == self.per, self.k


def patch_pieces():
    out = []
    for b in range(BB):
        n = 0
        while n < NP:
            t, p = divmod(b * NP + n, TT)
            c = min(NP - n, TT - p)
            out.append((t, p, b, n, c))
            n += c
    return out


def tower(nc, x, tok_w, tok_b, gamma, beta, w_qkv, res_k, w_out, b_out, gate_w, gate_b, w1, b1, w2, b2,
          consts, scratch, out):
    ctx = ExitStack()
    with ctx:
        def sb(name, shape, dt=F32):
            return ctx.enter_context(nc.sbuf_tensor(name, shape, dt))

        def sem(name):
            return ctx.enter_context(nc.semaphore(name))

        bank = [ctx.enter_context(nc.psum_tensor(f"bank{i}", [128, 512], F32)) for i in range(8)]

        cn = sb("cn", [128, CN_W])
        ident = cn[:, 0:128]
        tokw_sb = sb("tokw_sb", [D, D])
        tokb_sb = sb("tokb_sb", [128, D])
        bout_sb = sb("bout_sb", [128, D])
        gam_sb = sb("gam_sb", [D, 1])
        bet_sb = sb("bet_sb", [D, 1])
        wqkv_sb = sb("wqkv_sb", [D, 3 * D])
        wout_sb = sb("wout_sb", [D, D])
        kraw = sb("kraw", [HEADS, KER])
        kpad = sb("kpad", [HEADS, 2 * NP + 1])
        band = sb("band", [128, HEADS, NS])
        bands = sb("bands", [128, HEADS, NS])
        gw_sb = sb("gw_sb", [D, EXPERTS])
        gb_sb = sb("gb_sb", [128, EXPERTS])
        w1_sb = sb("w1_sb", [D, EXPERTS, HID])
        w2_sb = sb("w2_sb", [128, 2 * EXPERTS, D])
        b1_rows = sb("b1_rows", [2 * EXPERTS, 128])
        b1_sb = sb("b1_sb", [128, 2 * EXPERTS])
        b2_sb = sb("b2_sb", [EXPERTS, D])

        resid = sb("resid", [TT, BLOCKS * TILES, D])
        vals = sb("vals", [128, BLOCKS * UN, D])
        gram = sb("gram", [128, BLOCKS * GR * SL, NY])
        colsum = sb("colsum", [128, BLOCKS * GR * SL])
        rowsum = sb("rowsum", [128, BLOCKS * GR * SL])

        pat = sb("pat", [TT, TILES, D])
        patT = sb("patT", [D, BTP])
        h0 = sb("h0", [TT, TILES, D])
        h0b = sb("h0b", [TT, TILES, D])
        x1 = sb("x1", [TT, TILES, D])
        nm = sb("nm", [TT, TILES, D])
        stats = sb("stats", [TT, TILES, 6])
        mv = sb("mv", [TT, TILES, 2])
        spare = sb("spare", [TT, 2])
        sd = sb("sd", [TT, 2, TILES])
        rstd = sb("rstd", [TT, 2, TILES])
        normT = sb("normT", [D, BB, HALF])
        qeo = sb("qeo", [D, BB, 2, NS])
        kT = sb("kT", [D, BB, NS])
        E = [sb(f"E{i}", [128, SL, NS]) for i in range(2)]
        X = [sb(f"X{i}", [128, SL, HALF]) for i in range(2)]
        XT = [sb(f"XT{i}", [128, SL, NY]) for i in range(2)]
        mx = [sb(f"mx{i}", [128, SL]) for i in range(2)]
        r0 = sb("r0", [128, SL])
        cs0 = sb("cs0", [128, SL])
        rs = [sb(f"rs{i}", [128, SL]) for i in range(2)]
        ri = [sb(f"ri{i}", [128, SL]) for i in range(2)]
        rx = [sb(f"rx{i}", [128, SL]) for i in range(2)]
        cmax = sb("cmax", [128, 1])
        den = sb("den", [128, 2])
        den2 = sb("den2", [128, 2])
        dprod = sb("dprod", [128, 1])
        drec = sb("drec", [128, 1])
        lamc = sb("lamc", [128, 1])

        P0 = [sb(f"P0{g}", [128, SL, NS]) for g in range(GR)]
        P0Z = [sb(f"P0Z{g}", [128, SL, NS]) for g in range(GR)]
        P = [sb(f"P{g}", [128, SL, NS]) for g in range(GR)]
        Y = [sb(f"Y{g}", [128, SL, NS]) for g in range(GR)]
        W = [sb(f"W{g}", [128, SL, NS]) for g in range(GR)]
        PZ = [sb(f"PZ{g}", [128, SL, NS]) for g in range(GR)]
        XTZ = PZ[0:2]
        WZ = [sb(f"WZ{g}", [128, SL, NS]) for g in range(GR)]
        T = [sb(f"T{g}", [128, SL, NS]) for g in range(GR)]
        vblk = sb("vblk", [128, UN, D])
        O = sb("O", [128, UN, D])
        OT = sb("OT", [D, BTP])

        xn = nm
        stats2, mv2, sd2, rstd2 = stats, mv, sd[:, 0, :], rstd[:, 0, :]
        xnT = sb("xnT", [D, BTP])
        lg = sb("lg", [TT, TILES, EXPERTS])
        top = sb("top", [TT, TILES, 8])
        topi = sb("topi", [TT, TILES, 8], U32)
        topf = sb("topf", [TT, TILES, 8])
        oh1 = sb("oh1", [TT, TILES, EXPERTS])
        oh2 = sb("oh2", [TT, TILES, EXPERTS])
        dl = sb("dl", [TT, TILES, EXPERTS])
        ex = sb("ex", [TT, TILES, EXPERTS])
        em = sb("em", [TT, TILES, EXPERTS])
        es = sb("es", [TT, TILES])
        er = sb("er", [TT, TILES])
        wt = sb("wt", [TT, TILES, EXPERTS])
        wT = sb("wT", [EXPERTS, BTP])
        hT = [[sb(f"hT{i}{f}", [128, BTP]) for f in range(2)] for i in range(2)]
        acc = sb("acc", [TT, TILES, D])
        outb = sb("outb", [TT, TILES, D])

        s_cn, s_wa, s_wb, s_wc = sem("s_cn"), sem("s_wa"), sem("s_wb"), sem("s_wc")
        s_kraw, s_kpad, s_scr, s_band, s_bands = sem("s_kraw"), sem("s_kpad"), sem("s_scr"), sem("s_band"), sem("s_bands")
        s_init, s_psum = sem("s_init"), sem("s_psum")
        s_pat, s_pt, s_patT, s_h, s_h0 = sem("s_pat"), sem("s_pt"), sem("s_patT"), sem("s_h"), sem("s_h0")
        s_mv, s_sd, s_x1, s_res = sem("s_mv"), sem("s_sd"), sem("s_x1"), sem("s_res")
        s_nm, s_nt, s_normT = sem("s_nm"), sem("s_nt"), sem("s_normT")
        s_q, s_k, s_v, s_qk, s_vals, s_vx = sem("s_q"), sem("s_k"), sem("s_v"), sem("s_qk"), sem("s_vals"), sem("s_vx")
        s_s, s_sub, s_ex, s_norm, s_x = sem("s_s"), sem("s_sub"), sem("s_ex"), sem("s_norm"), sem("s_x")
        s_xz, s_c0, s_mx = sem("s_xz"), sem("s_c0"), sem("s_mx")
        s_xt, s_xte, s_g, s_gram, s_cs = sem("s_xt"), sem("s_xte"), sem("s_g"), sem("s_gram"), sem("s_cs")
        s_d1, s_d2, s_hb = sem("s_d1"), sem("s_d2"), sem("s_hb")
        s_den, s_den2, s_lamc, s_dd, s_dmax, s_es = (sem("s_den"), sem("s_den2"), sem("s_lamc"), sem("s_dd"),
                                                      sem("s_dmax"), sem("s_es"))
        s_p0 = [sem(f"s_p0{g}") for g in range(GR)]
        s_p = [sem(f"s_p{g}") for g in range(GR)]
        s_pp = [sem(f"s_pp{g}") for g in range(GR)]
        s_w = [sem(f"s_w{g}") for g in range(GR)]
        s_pz = [sem(f"s_pz{g}") for g in range(GR)]
        s_wz = [sem(f"s_wz{g}") for g in range(GR)]
        s_t = [sem(f"s_t{g}") for g in range(GR)]
        s_ww = [sem(f"s_ww{g}") for g in range(GR)]
        s_y = [sem(f"s_y{g}") for g in range(GR)]
        s_r = [sem(f"s_r{g}") for g in range(GR)]
        s_o = [sem(f"s_o{g}") for g in range(GR)]
        s_vb, s_ot, s_OT, s_pr, s_h1 = sem("s_vb"), sem("s_ot"), sem("s_OT"), sem("s_pr"), sem("s_h1")
        s_b1t, s_b1 = sem("s_b1t"), sem("s_b1")
        s_mv2, s_sd2, s_xn, s_xnt, s_xnT = sem("s_mv2"), sem("s_sd2"), sem("s_xn"), sem("s_xnt"), sem("s_xnT")
        s_gt, s_dl, s_exg, s_wt, s_wtt, s_wT, s_b2, s_acc = (sem("s_gt"), sem("s_dl"), sem("s_exg"), sem("s_wt"),
                                                            sem("s_wtt"), sem("s_wT"), sem("s_b2"), sem("s_acc"))
        s_up, s_hT, s_dn, s_mix, s_d3, s_d4, s_out = (sem("s_up"), sem("s_hT"), sem("s_dn"), sem("s_mix"), sem("s_d3"),
                                               sem("s_d4"), sem("s_out"))
        N_WA, N_WC = 6, 6
        N_FIRST, N_INIT = 6, 11 + 3 * GR

        halves = [(0, NS), (HALF, HALF + NS)]
        pieces = patch_pieces()
        block = ctx.enter_context(nc.Block())

        def over_blocks(eng, body):
            body(0)
            with eng.Fori(1, BLOCKS - 1) as blk:
                body(blk)
            body(BLOCKS - 1)

        def rows3(ap, blk, n):
            return ap[:, bass.ds(blk * n, n), :]

        @block.sync
        def _(sp):
            def load_patches(blk):
                wait(sp, s_pt, blk)
                for t, p, b, n, c in pieces:
                    src = bass.AP(tensor=x.tensor, offset=(blk * BB + b) * (L * C) + n * STRIDE * C,
                                  ap=[[STRIDE * C, c], [1, D]])
                    sp.dma_start(pat[p:p + c, t, :], src).then_inc(s_pat, 16)

            load_patches(0)
            sp.dma_start(kraw[:, :], res_k.rearrange("h a k b -> h (a k b)")).then_inc(s_kraw, 16)
            sp.wait_ge(s_kpad, 2)
            sp.dma_start(scratch[:, :], kpad[:, :]).then_inc(s_scr, 16)
            sp.wait_ge(s_scr, 16)
            for lo, _ in halves:
                src = bass.AP(tensor=scratch.tensor, offset=0, ap=[[1, NS], [2 * NP + 1, HEADS], [1, NS]])
                sp.dma_start(band[lo:lo + NS, :, :], src).then_inc(s_band, 16)
            load_patches(1)
            with sp.Fori(2, BLOCKS) as blk:
                load_patches(blk)
            out_rows = out.rearrange("b n d -> (b n) d")

            def store(blk):
                sp.wait_ge(s_mix, 8 * blk + 8)
                sp.dma_start(out_rows[bass.ds(blk * BT, BT), :].rearrange("(t p) d -> p t d", p=TT),
                             outb[:, :, :]).then_inc(s_out, 16)

            store(0)
            with sp.Fori(1, BLOCKS) as blk:
                store(blk)
            sp.wait_ge(s_out, 16 * BLOCKS)

        @block.gpsimd
        def _(pool):
            for t in (normT[:, :, :], patT[:, BT:BTP], X[0][:, :, :], X[1][:, :, :], XTZ[0][:, :, :], XTZ[1][:, :, :]):
                pool.memset(t, 0.0).then_inc(s_init, 1)
            for t in (xnT[:, BT:BTP], OT[:, BT:BTP], wT[:, BT:BTP], hT[0][0][:, BT:BTP], hT[0][1][:, BT:BTP],
                      hT[1][0][:, BT:BTP], hT[1][1][:, BT:BTP]) + tuple(z[:, :, :] for z in P0Z + WZ + PZ[2:]):
                pool.memset(t, 0.0).then_inc(s_init, 1)
            pool.wait_ge(s_wa, 16 * N_WA)
            pool.wait_ge(s_pat, 16 * len(pieces))
            pool.dma_start(gw_sb[:, :], gate_w).then_inc(s_wc, 16)
            pool.dma_start(gb_sb[:, :], gate_b.partition_broadcast(128)).then_inc(s_wc, 16)
            pool.dma_start(w1_sb[:, :, :], w1.rearrange("e h f -> h e f")).then_inc(s_wc, 16)
            pool.dma_start(w2_sb[:, :, :], w2.rearrange("e (c f) h -> f (e c) h", c=2)).then_inc(s_wc, 16)
            pool.dma_start(b1_rows[:, :], b1.rearrange("e (c f) -> (e c) f", c=2)).then_inc(s_wc, 16)
            pool.dma_start(b2_sb[:, :], b2).then_inc(s_wc, 16)

            def residual(blk):
                pool.wait_ge(s_h0, blk + 1)
                pool.tensor_tensor(out=h0b[:, :, :], in0=h0[:, :, :],
                                   in1=bout_sb[0:TT, :].unsqueeze(1).broadcast_to([TT, TILES, D]),
                                   op=ALU.add).then_inc(s_hb, 1)
                pool.wait_ge(s_hb, blk + 1)
                pool.wait_ge(s_x1, blk + 1)
                pool.tensor_tensor(out=rows3(resid, blk, TILES), in0=h0b[:, :, :], in1=x1[:, :, :],
                                   op=ALU.add).then_inc(s_res, 1)

            def values(blk, g):
                i = blk * GR + g
                pool.wait_ge(s_vals, blk + 1)
                wait(pool, s_g, i - 1)
                src = vals[:, bass.ds(blk * UN, UN), 2 * DH * g:2 * DH * (g + 1)]
                pool.tensor_copy(XT[g % 2][:, :, NS:NY].rearrange("p (u a) d -> p u a d", a=2),
                                 src.rearrange("p u (a d) -> p u a d", a=2)).then_inc(s_vx, 1)

            def scale_rows(blk, g):
                i = blk * GR + g
                pool.wait_ge(s_norm, i + 1)
                wait(pool, s_xt, i - 1)
                pool.tensor_tensor(out=X[g % 2][:, :, 0:NS], in0=E[g % 2][:, :, :],
                                   in1=rx[g % 2][:, :].unsqueeze(2).broadcast_to([128, SL, NS]),
                                   op=ALU.mult).then_inc(s_x, 1)
                pool.tensor_tensor(out=rowsum[:, bass.ds(i * SL, SL)], in0=rs[g % 2][:, :],
                                   in1=ri[g % 2][:, :], op=ALU.mult).then_inc(s_d2, 1)

            pool.wait_ge(s_init, N_INIT)
            pool.wait_ge(s_wa, 16 * N_WA)
            residual(0)

            def body(blk, more=True):
                for g in range(GR):
                    scale_rows(blk, g)
                    values(blk, g)
                    if g == 2 and more:
                        residual(blk + 1)

            body(0)
            with pool.Fori(1, BLOCKS - 1) as blk:
                body(blk)
            body(BLOCKS - 1, False)

            pool.wait_ge(s_den, 2)
            pool.partition_all_reduce(den2[:, :], den[:, :], 128, RMAX).then_inc(s_den2, 1)

            def block_values(blk):
                for g in range(GR):
                    wait(pool, s_r[g], blk)
                    pool.tensor_copy(Y[g][:, :, :], rows3(gram, blk * GR + g, SL)[:, :, NY - NS:NY]).then_inc(s_y[g], 1)
                wait(pool, s_r[GR - 1], blk)
                pool.tensor_copy(vblk[:, :, :], rows3(vals, blk, UN)).then_inc(s_vb, 1)

            def next_p(blk):
                for g in range(GR):
                    wait(pool, s_t[g], ITERS * (blk - 1) + 1)
                    src = rows3(gram, blk * GR + g, SL)
                    scale = lamc[:, 0:1].unsqueeze(2).broadcast_to([128, SL, NS])
                    pool.tensor_tensor(out=P0[g][:, :, :], in0=src[:, :, 0:NS], in1=scale, op=ALU.mult).then_inc(s_p0[g], 1)
                    pool.tensor_tensor(out=P0Z[g][0:HALF, :, :], in0=src[0:HALF, :, 0:NS], in1=scale[0:HALF],
                                       op=ALU.mult).then_inc(s_p0[g], 1)

            block_values(0)
            pool.wait_ge(s_lamc, 1)
            with pool.Fori(1, BLOCKS) as blk:
                next_p(blk)
                block_values(blk)

        @block.scalar
        def _(act):
            act.dma_start(cn[:, :], consts).then_inc(s_cn, 16)
            act.dma_start(tokw_sb[:, :], tok_w).then_inc(s_wa, 16)
            act.dma_start(tokb_sb[:, :], tok_b.partition_broadcast(128)).then_inc(s_wa, 16)
            act.dma_start(gam_sb[:, :], gamma.unsqueeze(1)).then_inc(s_wa, 16)
            act.dma_start(bet_sb[:, :], beta.unsqueeze(1)).then_inc(s_wa, 16)
            act.dma_start(wqkv_sb[:, :], w_qkv).then_inc(s_wa, 16)
            act.dma_start(bout_sb[:, :], b_out.partition_broadcast(128)).then_inc(s_wa, 16)
            act.dma_start(wout_sb[:, :], w_out).then_inc(s_wb, 16)

            def patches(blk):
                act.wait_ge(s_pt, blk + 1)
                wait(act, s_h, blk)
                act.activation(patT[:, 0:BT], bank[0][:, 0:BT], ACT.Copy).then_inc(s_patT, 1)

            def roots(blk):
                act.wait_ge(s_mv, blk + 1)
                act.activation(sd[:, 0, :], mv[:, :, 1], ACT.Sqrt, bias=cn[0:TT, CN_EPS:CN_EPS + 1])
                act.activation(sd[:, 1, :], mv[:, :, 1], ACT.Sqrt, bias=cn[0:TT, CN_EPS2:CN_EPS2 + 1],
                               scale=1.0 + EPS).then_inc(s_sd, 1)

            def normed(blk):
                act.wait_ge(s_nt, blk + 1)
                wait(act, s_v, blk)
                act.activation(normT[:, :, 1:NS], bank[0][:, 0:BT].rearrange("p (b n) -> p b n", b=BB),
                               ACT.Identity, bias=bet_sb[:, 0:1], scale=gam_sb[:, 0:1]).then_inc(s_normT, 1)

            def queries_keys(blk):
                q = bank[2][:, 0:BW].rearrange("p (b n) -> p b n", b=BB)
                act.wait_ge(s_q, blk + 1)
                act.activation(qeo[:, :, 0, :], q, ACT.Copy, scale=cn[:, CN_ME:CN_ME + 1]).then_inc(s_qk, 1)
                act.activation(qeo[:, :, 1, :], q, ACT.Copy, scale=cn[:, CN_MO:CN_MO + 1]).then_inc(s_qk, 1)
                act.wait_ge(s_k, blk + 1)
                act.activation(kT[:, :, :], bank[3][:, 0:BW].rearrange("p (b n) -> p b n", b=BB),
                               ACT.Copy).then_inc(s_qk, 1)

            def values(blk):
                act.wait_ge(s_v, blk + 1)
                act.activation(rows3(vals, blk, UN), bank[0][:, :].rearrange("p (u d) -> p u d", u=UN),
                               ACT.Copy).then_inc(s_vals, 1)

            def exps(i, b):
                act.wait_ge(s_sub, i + 1)
                act.activation(E[b][:, :, :], E[b][:, :, :], ACT.Exp).then_inc(s_ex, 1)

            turned = bank[6][:, :].rearrange("p (s n) -> p s n", s=SL)[:, :, 0:NS]

            def xt_out(i, b):
                act.wait_ge(s_xt, i + 1)
                wait(act, s_cs, i - 1)
                wait(act, s_g, i - 1)
                act.activation(XT[b][:, :, 0:NS], turned, ACT.Copy).then_inc(s_xte, 1)

            def xt_over_zeros(i, b):
                act.activation(XTZ[b][0:HALF, :, :], turned[0:HALF], ACT.Copy).then_inc(s_xz, 1)

            def gram_out(i):
                act.wait_ge(s_g, i + 1)
                act.activation(rows3(gram, i, SL), bank[7][:, 0:SL * NY].rearrange("p (s n) -> p s n", s=SL),
                               ACT.Copy).then_inc(s_gram, 1)

            act.wait_ge(s_cn, 16)
            act.activation(spare[:, :], cn[0:TT, CN_EPS:CN_EPS + 2], ACT.Sqrt)
            act.wait_ge(s_wa, 16 * N_WA)
            act.wait_ge(s_init, N_FIRST)
            patches(0)
            roots(0)
            normed(0)
            queries_keys(0)
            values(0)
            patches(1)
            exps(0, 0)

            def body(blk, first=False, more=True, ahead=True):
                for g in range(GR):
                    i, late = blk * GR + g, not (first and g == 0)
                    if more and g == 3:
                        queries_keys(blk + 1)
                    if not (first and g < 2):
                        gram_out(i - 2)
                    if late:
                        xt_out(i - 1, (g - 1) % 2)
                        xt_over_zeros(i - 1, (g - 1) % 2)
                    if more and g == 1:
                        roots(blk + 1)
                    if more and g == 2:
                        normed(blk + 1)
                    if more and g == 3:
                        values(blk + 1)
                    if more or g < 3:
                        exps(i + 1, (g + 1) % 2)
                    if ahead and g == 3:
                        patches(blk + 2)

            body(0, True)
            with act.Fori(1, BLOCKS - 2) as blk:
                body(blk)
            body(BLOCKS - 2, ahead=False)
            body(BLOCKS - 1, more=False, ahead=False)
            last = BLOCKS * GR - 1
            gram_out(last - 1)
            xt_out(last, last % 2)
            xt_over_zeros(last, last % 2)
            gram_out(last)

            act.wait_ge(s_init, N_INIT)
            act.wait_ge(s_b1t, 1)
            act.activation(b1_sb[:, :], bank[6][:, 0:2 * EXPERTS], ACT.Copy).then_inc(s_b1, 1)
            act.wait_ge(s_lamc, 1)

            def first_p(blk):
                for g in range(GR):
                    src = rows3(gram, blk * GR + g, SL)
                    act.activation(P0[g][:, :, :], src[:, :, 0:NS], ACT.Copy, scale=lamc[:, 0:1]).then_inc(s_p0[g], 1)
                    act.activation(P0Z[g][0:HALF, :, :], src[0:HALF, :, 0:NS], ACT.Copy,
                                   scale=lamc[0:HALF, 0:1]).then_inc(s_p0[g], 1)

            def root2(blk):
                act.wait_ge(s_mv2, blk + 1)
                act.activation(sd2[:, :], mv2[:, :, 1], ACT.Sqrt, bias=cn[0:TT, CN_EPS:CN_EPS + 1]).then_inc(s_sd2, 1)

            def xn_out(blk, bk=0):
                act.wait_ge(s_xnt, blk + 1)
                wait(act, s_up, 16 * blk)
                act.activation(xnT[:, 0:BT], bank[bk][:, 0:BT], ACT.Copy).then_inc(s_xnT, 1)

            def gate_exp(blk):
                act.wait_ge(s_dl, blk + 1)
                act.activation(ex[:, :, :], dl[:, :, :], ACT.Exp).then_inc(s_exg, 1)

            def over_zeros(src, dst, sem_in, sem_out, count):
                for g in range(GR):
                    act.wait_ge(sem_in[g], count)
                    act.activation(dst[g][0:HALF, :, :], src[g][0:HALF, :, :], ACT.Copy).then_inc(sem_out[g], 1)

            def attention_rows(blk, bk=4):
                act.wait_ge(s_ot, blk + 1)
                act.activation(OT[:, 0:BT].rearrange("p (b n) -> p b n", b=BB),
                               bank[bk][:, :].rearrange("p (b n) -> p b n", b=BB)[:, :, 1:NS],
                               ACT.Copy).then_inc(s_OT, 1)

            def b_body(blk, before=True, last=False):
                over_zeros(W, WZ, s_w, s_wz, blk * ITERS + 1)
                if before:
                    attention_rows(blk - 1)
                over_zeros(P, PZ, s_p, s_pz, blk * ITERS + 1)
                if last:
                    root2(0)
                    over_zeros(W, WZ, s_w, s_wz, blk * ITERS + 2)
                    xn_out(0, 6)
                    over_zeros(P, PZ, s_p, s_pz, blk * ITERS + 2)
                    gate_exp(0)
                with act.Fori(2 if last else 1, ITERS) as k:
                    over_zeros(W, WZ, s_w, s_wz, blk * ITERS + k + 1)
                    over_zeros(P, PZ, s_p, s_pz, blk * ITERS + k + 1)

            def relus(blk, e):
                for f in range(2):
                    j = blk * 16 + 2 * e + f
                    act.wait_ge(s_up, j + 1)
                    wait(act, s_dn, blk * 8 + e - 1)
                    act.activation(hT[e % 2][f][:, 0:BT], bank[4 + f][:, 0:BT], ACT.Relu,
                                   bias=b1_sb[:, 2 * e + f:2 * e + f + 1]).then_inc(s_hT, 1)

            first_p(0)
            b_body(0, False)
            with act.Fori(1, BLOCKS - 1) as blk:
                b_body(blk)
            b_body(BLOCKS - 1, last=True)

            def c_body(blk, more=True, first=False):
                relus(blk, 0)
                if first:
                    attention_rows(BLOCKS - 1, 0)
                relus(blk, 1)
                act.wait_ge(s_wtt, blk + 1)
                act.activation(wT[:, 0:BT], bank[2][0:EXPERTS, 0:BT], ACT.Copy).then_inc(s_wT, 1)
                relus(blk, 2)
                relus(blk, 3)
                if more:
                    root2(blk + 1)
                for e in range(4, EXPERTS):
                    relus(blk, e)
                if more:
                    xn_out(blk + 1)
                    gate_exp(blk + 1)

            c_body(0, first=True)
            with act.Fori(1, BLOCKS - 1) as blk:
                c_body(blk)
            c_body(BLOCKS - 1, False)

        @block.vector
        def _(dve):
            for bk in bank:
                dve.memset(bk[:, :], 0.0).then_inc(s_psum, 1)
            dve.memset(kpad[:, :], 0.0).then_inc(s_kpad, 1)
            dve.wait_ge(s_kraw, 16)
            dve.wait_ge(s_kpad, 1)
            first = NP - KER // 2
            dve.tensor_copy(kpad[:, first:first + KER], kraw[:, :]).then_inc(s_kpad, 1)
            a1 = Steps(dve, s_d1, 2, (s_cn, 16))
            a2 = Steps(dve, s_dd, 4, (s_cn, 16))
            dve.wait_ge(s_cn, 16)
            dve.wait_ge(s_wa, 16 * N_WA)

            def ln_stats(src, st, m, chain):
                for t in range(TILES):
                    ins = dve.bn_stats(st[:, t, :], src(t))
                chain.done(ins, True)
                for t in range(TILES):
                    ins = dve.bn_aggr(m[:, t, :], st[:, t, :])
                return ins

            def ln_apply(dst, src, m, r):
                for t in range(TILES):
                    ins = dve.tensor_scalar(dst[:, t, :], src(t), m[:, t, 0:1], r[:, t:t + 1],
                                            ALU.subtract, ALU.mult)
                return ins

            def embed(blk):
                a1.start(blk)
                dve.wait_ge(s_h, blk + 1)
                wait(dve, s_res, blk)
                dve.tensor_tensor(out=h0[:, :, :],
                                  in0=bank[1][0:TT, 0:TILES * D].rearrange("p (t d) -> p t d", t=TILES),
                                  in1=tokb_sb[0:TT, :].unsqueeze(1).broadcast_to([TT, TILES, D]),
                                  op=ALU.add).then_inc(s_h0, 1)
                dve.wait_ge(s_h0, blk + 1)
                ln_stats(lambda t: h0[:, t, :], stats, mv, a1).then_inc(s_mv, 1)

            def norms(blk):
                dve.wait_ge(s_sd, blk + 1)
                a1.done(dve.reciprocal(rstd[:, :, :], sd[:, :, :]))
                wait(dve, s_nt, blk)
                ln_apply(nm, lambda t: h0[:, t, :], mv, rstd[:, 1, :]).then_inc(s_nm, 1)
                ln_apply(x1, lambda t: h0[:, t, :], mv, rstd[:, 0, :]).then_inc(s_x1, 1)
                a1.end()

            def subtract(i, b):
                S = bank[4 + b][:, 0:BW].rearrange("p (s n) -> p s n", s=SL)
                dve.wait_ge(s_s, i + 1)
                dve.reduce_max(mx[b][:, :], S, AX.X).then_inc(s_mx, 1)
                dve.wait_ge(s_mx, i + 1)
                wait(dve, s_x, i - 1)
                dve.tensor_tensor(out=E[b][:, :, :], in0=S,
                                  in1=mx[b][:, :].unsqueeze(2).broadcast_to([128, SL, NS]),
                                  op=ALU.subtract).then_inc(s_sub, 1)

            def normalise(i, b):
                e = E[b]
                a2.start(i)
                dve.wait_ge(s_ex, i + 1)
                wait(dve, s_d2, i - 1)
                a2.done(dve.reduce_sum(r0[:, :], e[:, :, :], AX.X))
                a2.done(dve.scalar_tensor_tensor(out=rs[b][:, :], in0=e[:, :, 0], scalar=float(PAD - 1),
                                                 in1=r0[:, :], op0=ALU.mult, op1=ALU.add))
                a2.done(dve.reciprocal(ri[b][:, :], rs[b][:, :]))
                a2.done(dve.tensor_scalar(rx[b][:, :], ri[b][:, :], cn[:, CN_ROW:CN_ROW + 1], None, ALU.mult))
                dve.tensor_scalar(e[:, :, 0], e[:, :, 0], PADW, None, ALU.mult).then_inc(s_norm, 1)
                a2.end()

            def columns(i, b):
                dve.wait_ge(s_xte, i + 1)
                dve.reduce_sum(cs0[:, :], XT[b][:, :, 0:NS], AX.X).then_inc(s_c0, 1)
                dve.wait_ge(s_c0, i + 1)
                dve.scalar_tensor_tensor(out=colsum[:, bass.ds(i * SL, SL)], in0=XT[b][:, :, 0],
                                         scalar=PADW - 1.0, in1=cs0[:, :], op0=ALU.mult,
                                         op1=ALU.add).then_inc(s_cs, 1)
                dve.wait_ge(s_cs, i + 1)

            def body(blk, first=False, more=True):
                for g in range(GR):
                    i = blk * GR + g
                    normalise(i, g % 2)
                    if more or g < 3:
                        subtract(i + 1, (g + 1) % 2)
                    if not (first and g == 0):
                        columns(i - 1, (g - 1) % 2)
                    if more and g == 0:
                        embed(blk + 1)
                    if more and g == 1:
                        norms(blk + 1)

            embed(0)
            norms(0)
            subtract(0, 0)
            body(0, True)
            with dve.Fori(1, BLOCKS - 1) as blk:
                body(blk)
            body(BLOCKS - 1, more=False)
            columns(BLOCKS * GR - 1, (GR - 1) % 2)

            dve.wait_ge(s_vals, BLOCKS)
            dve.wait_ge(s_qk, 3 * BLOCKS)
            for g in range(GR):
                dve.memset(bank[g][:, :], 0.0).then_inc(s_psum, 1)
            dve.reduce_max(cmax[:, :], colsum[:, :], AX.X).then_inc(s_dmax, 1)
            dve.wait_ge(s_d2, BLOCKS * GR)
            dve.reduce_max(den[:, 1:2], rowsum[:, :], AX.X).then_inc(s_den, 1)
            dve.wait_ge(s_dmax, 1)
            dve.tensor_scalar(den[:, 0:1], cmax[:, :], cn[:, CN_COL:CN_COL + 1], None, ALU.mult).then_inc(s_den, 1)
            dve.wait_ge(s_den2, 1)
            dve.tensor_tensor(out=dprod[:, :], in0=den2[:, 0:1], in1=den2[:, 1:2], op=ALU.mult).then_inc(s_dmax, 1)
            dve.wait_ge(s_dmax, 2)
            dve.reciprocal(drec[:, :], dprod[:, :]).then_inc(s_dmax, 1)
            dve.wait_ge(s_dmax, 3)
            dve.tensor_scalar(lamc[:, :], drec[:, :], LAM, None, ALU.mult).then_inc(s_lamc, 1)
            dve.wait_ge(s_band, 16 * 2)
            for lo, hi in halves:
                dve.tensor_scalar(bands[lo:hi, :, :], band[lo:hi, :, ::-1], LAM, None, ALU.mult).then_inc(s_bands, 1)

            def psum3(k, n):
                return bank[k][:, 0:SL * n].rearrange("p (s n) -> p s n", s=SL)

            def step(blk, k, src):
                c = blk * ITERS + k
                for g in range(GR):
                    dve.wait_ge(s_pp[g], c + 1)
                    dve.scalar_tensor_tensor(out=W[g][:, :, :], in0=psum3(g, NS), scalar=S_SCALE,
                                             in1=src[g][:, :, :], op0=ALU.mult, op1=ALU.subtract).then_inc(s_w[g], 1)
                    dve.wait_ge(s_w[g], c + 1)
                    dve.scalar_tensor_tensor(out=T[g][:, :, :], in0=src[g][:, :, :], scalar=T_IN, in1=W[g][:, :, :],
                                             op0=ALU.mult, op1=ALU.subtract).then_inc(s_t[g], 1)
                for g in range(GR):
                    dve.wait_ge(s_ww[g], c + 1)
                    dve.wait_ge(s_t[g], c + 1)
                    dve.scalar_tensor_tensor(out=P[g][:, :, :], in0=T[g][:, :, :], scalar=T_OUT, in1=psum3(g, NS),
                                             op0=ALU.mult, op1=ALU.subtract).then_inc(s_p[g], 1)

            def h1(blk, bk=5):
                dve.wait_ge(s_pr, blk + 1)
                r = rows3(resid, blk, TILES)
                dve.tensor_tensor(out=r, in0=bank[bk][0:TT, 0:TILES * D].rearrange("p (t d) -> p t d", t=TILES),
                                  in1=r, op=ALU.add).then_inc(s_h1, 1)

            c1 = Steps(dve, s_d3, 2, (s_cn, 16))
            c2 = Steps(dve, s_d4, 8, (s_cn, 16))

            def third_stats(blk):
                c1.start(blk)
                r = rows3(resid, blk, TILES)
                ln_stats(lambda t: r[:, t, :], stats2, mv2, c1).then_inc(s_mv2, 1)

            def third_norm(blk):
                r = rows3(resid, blk, TILES)
                dve.wait_ge(s_sd2, blk + 1)
                c1.done(dve.reciprocal(rstd2[:, :], sd2[:, :]))
                wait(dve, s_xnt, blk)
                ln_apply(xn, lambda t: r[:, t, :], mv2, rstd2).then_inc(s_xn, 1)
                c1.end()

            def every(ap, n):
                return ap.unsqueeze(2).broadcast_to([TT, TILES, n])

            def gate(blk, bk=1):
                c2.start(blk)
                dve.wait_ge(s_gt, blk + 1)
                c2.done(dve.tensor_tensor(
                    out=lg[:, :, :], in0=bank[bk][0:TT, 0:TILES * EXPERTS].rearrange("p (t e) -> p t e", t=TILES),
                    in1=gb_sb[0:TT, :].unsqueeze(1).broadcast_to([TT, TILES, EXPERTS]), op=ALU.add), True)
                for t in range(TILES):
                    ins = dve.max(top[:, t, :], lg[:, t, :])
                c2.done(ins)
                dve.tensor_tensor(out=dl[:, :, :], in0=lg[:, :, :], in1=every(top[:, :, 0], EXPERTS),
                                  op=ALU.subtract).then_inc(s_dl, 1)
                for t in range(TILES):
                    ins = dve.max_index(topi[:, t, :], top[:, t, :], lg[:, t, :])
                c2.done(ins)
                c2.done(dve.tensor_copy(topf[:, :, :], topi[:, :, :]))
                places = cn[0:TT, CN_IOTA:CN_IOTA + EXPERTS].unsqueeze(1).broadcast_to([TT, TILES, EXPERTS])
                dve.tensor_tensor(out=oh1[:, :, :], in0=places, in1=every(topf[:, :, 0], EXPERTS), op=ALU.is_equal)
                c2.done(dve.tensor_tensor(out=oh2[:, :, :], in0=places, in1=every(topf[:, :, 1], EXPERTS),
                                          op=ALU.is_equal))
                c2.done(dve.tensor_tensor(out=oh1[:, :, :], in0=oh1[:, :, :], in1=oh2[:, :, :], op=ALU.add))
                dve.wait_ge(s_exg, blk + 1)
                c2.done(dve.tensor_tensor(out=em[:, :, :], in0=ex[:, :, :], in1=oh1[:, :, :], op=ALU.mult))
                dve.reduce_sum(es[:, :], em[:, :, :], AX.X).then_inc(s_es, 1)
                dve.wait_ge(s_es, blk + 1)
                c2.done(dve.reciprocal(er[:, :], es[:, :]))
                c2.end()

            def gate_weights(blk):
                wait(dve, s_mix, 8 * blk)
                dve.tensor_tensor(out=wt[:, :, :], in0=em[:, :, :], in1=every(er[:, :], EXPERTS),
                                  op=ALU.mult).then_inc(s_wt, 1)

            def attention_out(blk):
                for g in range(GR):
                    dve.wait_ge(s_r[g], blk + 1)
                    dve.tensor_scalar(
                        O[:, :, 2 * DH * g:2 * DH * (g + 1)].rearrange("p u (a d) -> p u a d", a=2),
                        bank[4 + g][:, 0:BW].rearrange("p (u a n) -> p u a n", u=UN, a=2)[:, :, :, NS - DH:NS],
                        1.0 / LAM, None, ALU.mult).then_inc(s_o[g], 1)

            def b_body(blk, before=True, last=False):
                step(blk, 0, P0)
                if before:
                    h1(blk - 1)
                if last:
                    third_stats(0)
                    third_norm(0)
                    step(blk, 1, P)
                    gate(0, 7)
                    gate_weights(0)
                with dve.Fori(2 if last else 1, ITERS) as k:
                    step(blk, k, P)
                attention_out(blk)

            b_body(0, False)
            with dve.Fori(1, BLOCKS - 1) as blk:
                b_body(blk)
            b_body(BLOCKS - 1, last=True)

            def add_bias(blk):
                dve.wait_ge(s_b2, blk + 1)
                dve.wait_ge(s_mix, 8 * blk + 4)
                dve.tensor_tensor(out=acc[:, :, :], in0=bank[3][0:TT, 0:TILES * D].rearrange("p (t d) -> p t d", t=TILES),
                                  in1=acc[:, :, :], op=ALU.add).then_inc(s_acc, 1)

            def mix(blk, e):
                j = blk * EXPERTS + e
                dve.wait_ge(s_dn, j + 1)
                before = acc
                if e == 0:
                    dve.wait_ge(s_wt, blk + 1)
                    before = rows3(resid, blk, TILES)
                elif e == 4:
                    dve.wait_ge(s_acc, blk + 1)
                else:
                    dve.wait_ge(s_mix, j)
                dst = acc
                if e == EXPERTS - 1:
                    dst = outb
                    wait(dve, s_out, 16 * blk)
                y = bank[6 + e % 2][0:TT, 0:TILES * D].rearrange("p (t d) -> p t d", t=TILES)
                for t in range(TILES):
                    ins = dve.scalar_tensor_tensor(out=dst[:, t, :], in0=y[:, t, :], scalar=wt[:, t, e:e + 1],
                                                   in1=before[:, t, :], op0=ALU.mult, op1=ALU.add)
                ins.then_inc(s_mix, 1)

            def c_body(blk, more=True, first=False):
                mix(blk, 0)
                if first:
                    h1(BLOCKS - 1, 1)
                    dve.wait_ge(s_h1, BLOCKS)
                if more:
                    third_stats(blk + 1)
                for e in range(1, 4):
                    mix(blk, e)
                add_bias(blk)
                if more:
                    third_norm(blk + 1)
                for e in range(4, 7):
                    mix(blk, e)
                if more:
                    gate(blk + 1)
                mix(blk, 7)
                if more:
                    gate_weights(blk + 1)

            c_body(0, first=True)
            with dve.Fori(1, BLOCKS - 1) as blk:
                c_body(blk)
            c_body(BLOCKS - 1, False)

        @block.tensor
        def _(pe):
            def mm(out, lhsT, rhs, start=True, stop=True):
                return pe.matmul(out, lhsT, rhs, start=start, stop=stop, skip_group_check=True)

            met = (s_cn, 16)
            pe.wait_ge(s_psum, 8)
            pe.wait_ge(s_init, N_FIRST)
            pe.wait_ge(s_cn, 16)

            def patches(blk):
                pe.wait_ge(s_pat, 16 * len(pieces) * blk + 16 * len(pieces))
                wait(pe, s_vals, blk)
                for t in range(TILES):
                    ins = pe.transpose(bank[0][:, t * TT:(t + 1) * TT], pat[:, t, :], ident[0:TT, 0:TT])
                ins.then_inc(s_pt, 1)

            def embed(blk):
                pe.wait_ge(s_patT, blk + 1)
                wait(pe, s_h0, blk)
                for t in range(TILES):
                    ins = mm(bank[1][:, t * D:(t + 1) * D], patT[:, t * TT:t * TT + 128], tokw_sb[:, :])
                ins.then_inc(s_h, 1)

            def normed(blk):
                pe.wait_ge(s_nm, blk + 1)
                for t in range(TILES):
                    ins = pe.transpose(bank[0][:, t * TT:(t + 1) * TT], nm[:, t, :], ident[0:TT, 0:TT])
                ins.then_inc(s_nt, 1)

            def qkv(blk):
                pe.wait_ge(s_normT, blk + 1)
                rhs = normT[:, :, 0:NS]
                mm(bank[2][:, 0:BW].rearrange("p (b n) -> p b n", b=BB), wqkv_sb[:, 0:D], rhs).then_inc(s_q, 1)
                mm(bank[3][:, 0:BW].rearrange("p (b n) -> p b n", b=BB), wqkv_sb[:, D:2 * D], rhs).then_inc(s_k, 1)
                for u in range(UN):
                    ins = mm(bank[0][:, u * D:(u + 1) * D], normT[:, 2 * u:2 * u + 2, :].rearrange("p b n -> p (b n)"),
                             wqkv_sb[:, 2 * D:3 * D])
                ins.then_inc(s_v, 1)

            def scores(blk, g):
                i = blk * GR + g
                if g == 0:
                    pe.wait_ge(s_qk, 3 * blk + 3)
                wait(pe, s_sub, i - 1)
                r = slice(32 * g, 32 * g + 32)
                for b in range(BB):
                    for a, (lo, hi) in enumerate(halves):
                        ins = pe.matmul(bank[4 + g % 2][lo:hi, b * NS:(b + 1) * NS], qeo[r, b, a, :], kT[r, b, :],
                                        start=True, stop=True, skip_group_check=True, tile_position=(32 * g, lo))
                ins.then_inc(s_s, 1)

            def turn(i, b):
                pe.wait_ge(s_x, i + 1)
                wait(pe, s_xz, i)
                for u in range(UN):
                    ins = pe.transpose(bank[6][:, u * 128:(u + 1) * 128],
                                       X[b][:, 2 * u:2 * u + 2, :].rearrange("p b n -> p (b n)"), ident)
                ins.then_inc(s_xt, 1)

            def pair(out_bank, s, n, t, tz, rhs, **flags):
                mm(out_bank[0:NS, s * n:(s + 1) * n], tz[:, s, :], rhs, **flags)
                return mm(out_bank[HALF:HALF + NS, s * n:(s + 1) * n], t[HALF:128, s, 0:NS], rhs[HALF:128, :], **flags)

            def products(i, b):
                wait_apart(pe, met, (s_xz, i + 1), (s_vx, i + 1), (s_gram, i))
                for s in range(SL):
                    ins = pair(bank[7], s, NY, XT[b], XTZ[b], XT[b][:, s, :])
                ins.then_inc(s_g, 1)

            def keep_warm():
                for _ in range(WARM_A):
                    mm(bank[3][:, 0:3 * D], ident, wqkv_sb[:, :])

            pe.wait_ge(s_wa, 16 * N_WA)
            patches(0)
            embed(0)
            normed(0)
            qkv(0)
            patches(1)
            scores(0, 0)

            def body(blk, first=False, more=True, ahead=True):
                for g in range(GR):
                    i, late = blk * GR + g, not (first and g == 0)
                    if late:
                        turn(i - 1, (g - 1) % 2)
                    if g < 3:
                        scores(blk, g + 1)
                    elif more:
                        scores(blk + 1, 0)
                    if more and g == 0:
                        embed(blk + 1)
                    if more and g == 2:
                        normed(blk + 1)
                    if late:
                        products(i - 1, (g - 1) % 2)
                    if more and g == 2:
                        qkv(blk + 1)
                    if ahead and g == 3:
                        patches(blk + 2)
                    if g != 2:
                        keep_warm()

            body(0, True)
            with pe.Fori(1, BLOCKS - 2) as blk:
                body(blk)
            body(BLOCKS - 2, ahead=False)
            body(BLOCKS - 1, more=False, ahead=False)
            last = BLOCKS * GR - 1
            turn(last, last % 2)
            products(last, last % 2)

            pe.wait_ge(s_wc, 16 * N_WC)
            pe.wait_ge(s_wb, 16)
            pe.transpose(bank[6][:, 0:2 * EXPERTS], b1_rows[:, :], ident[0:16, 0:16]).then_inc(s_b1t, 1)
            for _ in range(WARM_B):
                mm(bank[5][:, :], ident, w1_sb[:, 0:2, :].rearrange("p e f -> p (e f)"))

            def squares(g, t, tz):
                for s in range(SL):
                    ins = pair(bank[g], s, NS, t, tz, t[:, s, :])
                return ins

            def p_squares(blk, k):
                for g in range(GR):
                    wait_apart(pe, met, (s_pz[g], blk * ITERS + k))
                    squares(g, P[g], PZ[g]).then_inc(s_pp[g], 1)

            def w_squares(blk, k):
                for g in range(GR):
                    wait_apart(pe, met, (s_wz[g], blk * ITERS + k + 1))
                    squares(g, W[g], WZ[g]).then_inc(s_ww[g], 1)

            def first_squares(blk):
                for g in range(GR):
                    wait_apart(pe, met, (s_p0[g], 2 * blk + 2))
                    squares(g, P0[g], P0Z[g]).then_inc(s_pp[g], 1)

            def turn_out(blk, bk=4):
                for g in range(GR):
                    pe.wait_ge(s_o[g], blk + 1)
                for u in range(UN):
                    ins = pe.transpose(bank[bk][:, u * 128:(u + 1) * 128], O[:, u, :], ident)
                ins.then_inc(s_ot, 1)

            def project(blk, bk=5):
                pe.wait_ge(s_OT, blk + 1)
                for t in range(TILES):
                    ins = mm(bank[bk][:, t * D:(t + 1) * D], OT[:, t * TT:t * TT + 128], wout_sb[:, :])
                ins.then_inc(s_pr, 1)

            def third_norm(blk, bk=0):
                pe.wait_ge(s_xn, blk + 1)
                for t in range(TILES):
                    ins = pe.transpose(bank[bk][:, t * TT:(t + 1) * TT], xn[:, t, :], ident[0:TT, 0:TT])
                ins.then_inc(s_xnt, 1)

            def gate(blk, bk=1):
                pe.wait_ge(s_xnT, blk + 1)
                for t in range(TILES):
                    ins = mm(bank[bk][:, t * EXPERTS:(t + 1) * EXPERTS], xnT[:, t * TT:t * TT + 128], gw_sb[:, :])
                ins.then_inc(s_gt, 1)

            def results(blk):
                for g in range(GR):
                    wait_apart(pe, met, (s_pz[g], ITERS * blk + ITERS), (s_y[g], blk + 1), (s_vb, blk + 1),
                               (s_h1, blk), (s_o[g], blk))
                    for s in range(SL):
                        pair(bank[4 + g], s, NS, P[g], PZ[g], Y[g][:, s, :], start=(s == 0), stop=False)
                    for lo, hi in halves:
                        for a in range(2):
                            h = 2 * g + a
                            dst = bank[4 + g][lo:hi, 0:BW].rearrange("p (u a n) -> p u a n", u=UN, a=2)
                            ins = mm(dst[:, :, a, NS - DH:NS], bands[lo:hi, h, :], vblk[lo:hi, :, h * DH:(h + 1) * DH],
                                     start=False, stop=True)
                    ins.then_inc(s_r[g], 1)

            def b_body(blk, before=True, last=False):
                first_squares(blk)
                if before:
                    turn_out(blk - 1)
                w_squares(blk, 0)
                if before:
                    project(blk - 1)
                if last:
                    p_squares(blk, 1)
                    third_norm(0, 6)
                    w_squares(blk, 1)
                    gate(0, 7)
                with pe.Fori(2 if last else 1, ITERS) as k:
                    p_squares(blk, k)
                    w_squares(blk, k)
                if last:
                    pe.wait_ge(s_dl, 1)
                results(blk)

            pe.wait_ge(s_bands, 2)
            pe.wait_ge(s_init, N_INIT)
            pe.wait_ge(s_psum, 8 + GR)
            b_body(0, False)
            with pe.Fori(1, BLOCKS - 1) as blk:
                b_body(blk)
            b_body(BLOCKS - 1, last=True)

            def up(blk, e):
                for f in range(2):
                    wait(pe, s_hT, blk * 16 + 2 * e + f - 1)
                    mm(bank[4 + f][:, 0:BT], w1_sb[:, e, f * 128:(f + 1) * 128], xnT[:, 0:BT]).then_inc(s_up, 1)

            def weights(blk):
                pe.wait_ge(s_wt, blk + 1)
                for t in range(TILES):
                    ins = pe.transpose(bank[2][0:EXPERTS, t * TT:(t + 1) * TT], wt[:, t, :], ident[0:TT, 0:TT])
                ins.then_inc(s_wtt, 1)

            def second_bias(blk):
                pe.wait_ge(s_wT, blk + 1)
                wait(pe, s_acc, blk)
                for t in range(TILES):
                    ins = mm(bank[3][:, t * D:(t + 1) * D], wT[:, t * TT:t * TT + 128], b2_sb[:, :])
                ins.then_inc(s_b2, 1)

            def down(blk, e):
                j = blk * EXPERTS + e
                pe.wait_ge(s_hT, 2 * j + 2)
                wait(pe, s_mix, j - 1)
                for t in range(TILES):
                    for f in range(2):
                        ins = mm(bank[6 + e % 2][:, t * D:(t + 1) * D], hT[e % 2][f][:, t * TT:t * TT + 128],
                                 w2_sb[:, 2 * e + f, :], start=(f == 0), stop=(f == 1))
                ins.then_inc(s_dn, 1)

            def c_body(blk, more=True, first=False):
                if first:
                    for g in range(2):
                        pe.wait_ge(s_o[g], BLOCKS)
                up(blk, 0)
                if first:
                    turn_out(BLOCKS - 1, 0)
                up(blk, 1)
                if first:
                    project(BLOCKS - 1, 1)
                down(blk, 0)
                weights(blk)
                up(blk, 2)
                second_bias(blk)
                down(blk, 1)
                for e in range(3, EXPERTS):
                    up(blk, e)
                    if more and e == 6:
                        third_norm(blk + 1)
                    down(blk, e - 1)
                if more:
                    gate(blk + 1)
                down(blk, EXPERTS - 1)

            c_body(0, first=True)
            with pe.Fori(1, BLOCKS - 1) as blk:
                c_body(blk)
            c_body(BLOCKS - 1, False)


_INS = ['x', 'L0_tok_W', 'L0_tok_b', 'L0_attn_gamma', 'L0_attn_beta', 'L0_attn_w_qkv', 'L0_attn_res_kernel',
        'L0_attn_w_out', 'L0_attn_b_out', 'L0_ffn_gate_w', 'L0_ffn_gate_b', 'L0_ffn_w1', 'L0_ffn_b1',
        'L0_ffn_w2', 'L0_ffn_b2']


def shape_constants():
    import numpy as np
    cn = np.zeros((128, CN_W), np.float32)
    cn[:, 0:128] = np.eye(128)
    p = np.arange(128)
    cn[:, CN_ME] = np.where(p // DH % 2 == 0, DH ** -0.5, 0.0)
    cn[:, CN_MO] = np.where(p // DH % 2 == 1, DH ** -0.5, 0.0)
    cn[:, CN_ROW] = np.where(p % HALF == 0, PADW, 1.0)
    cn[:, CN_COL] = np.where(p % HALF == 0, 1.0 / PADW, np.where(p % HALF < NS, 1.0, 0.0))
    cn[:, CN_EPS] = EPS
    cn[:, CN_EPS2] = EPS ** 2
    cn[:, CN_IOTA:CN_IOTA + EXPERTS] = np.arange(EXPERTS)
    return cn


def kernel(**inputs):
    import numpy as _np
    import concourse.bacc as _bacc
    from concourse.bass_utils import run_bass_kernel_spmd as _run

    nc = _bacc.Bacc("TRN2", target_bir_lowering=False, num_devices=1)
    arrays, args = {}, []
    for name in _INS:
        a = _np.ascontiguousarray(inputs[name])
        arrays[f"in_{name}"] = a
        args.append(nc.dram_tensor(f"in_{name}", a.shape, F32, kind="ExternalInput").ap())
    arrays["in_consts"] = shape_constants()
    consts = nc.dram_tensor("in_consts", (128, CN_W), F32, kind="ExternalInput").ap()
    scratch = nc.dram_tensor("scratch", (HEADS, 2 * NP + 1), F32, kind="Internal").ap()
    out = nc.dram_tensor("out", (B, NP, D), F32, kind="ExternalOutput").ap()
    tower(nc, *args, consts, scratch, out)
    r = _run(nc, [arrays], core_ids=[0])
    return r.results[0]["out"]
```
